# Optimizing a Trainium2 kernel written in Bass

```python
import numpy as np
import jax
import jax.numpy as jnp

def _softmax(x, axis=-1):
    return jax.nn.softmax(x, axis=axis)

def _gelu(x):
    return jax.nn.gelu(x, approximate=True)

def _silu(x):
    return jax.nn.silu(x)

def _sigmoid(x):
    return jax.nn.sigmoid(x)

def _layernorm(x, axis=-1, eps=1e-05):
    m = jnp.mean(x, axis=axis, keepdims=True)
    v = jnp.var(x, axis=axis, keepdims=True)
    return (x - m) / jnp.sqrt(v + eps)

def _scatter_add(tgt, idx, src, axis=0):
    return tgt.at[idx].add(src)

def _segment_sum(src, seg, n):
    return jax.ops.segment_sum(src, seg, n)
kernel_name = 'mk_dlrm_tower_d1_rec_r8_4440ab'

def setup_inputs(seed: int=0):
    np.random.seed(seed)
    _w = jnp.asarray

    def _rec_inputs():
        import jax
        import jax.numpy as jnp
        _tk = jax.random.key(seed)
        dense_ctx = jax.random.normal(jax.random.fold_in(_tk, 190), (512, 16), jnp.float32)
        ids = jnp.stack([jax.random.randint(jax.random.fold_in(_tk, 200 + f), (512,), 0, v, jnp.int32) for f, v in enumerate([12500, 125000, 1250, 12500, 125000, 1250, 12500, 12500, 12500, 125000, 125000, 12500, 12500, 125000, 1250, 1250, 1250, 12500, 1000, 1000, 1000, 1000, 12500, 1250, 12500, 1000, 1000, 12500, 1000, 1000, 1250, 125000, 12500, 12500, 12500, 1250, 1000, 1250, 1000, 1000])], axis=1)
        tbl_0 = 0.05 * jax.random.normal(jax.random.fold_in(_tk, 500 + 0), (12500, 32), jnp.float32)
        tbl_1 = 0.05 * jax.random.normal(jax.random.fold_in(_tk, 500 + 1), (125000, 32), jnp.float32)
        tbl_2 = 0.05 * jax.random.normal(jax.random.fold_in(_tk, 500 + 2), (1250, 32), jnp.float32)
        tbl_3 = 0.05 * jax.random.normal(jax.random.fold_in(_tk, 500 + 3), (12500, 32), jnp.float32)
        tbl_4 = 0.05 * jax.random.normal(jax.random.fold_in(_tk, 500 + 4), (125000, 32), jnp.float32)
        tbl_5 = 0.05 * jax.random.normal(jax.random.fold_in(_tk, 500 + 5), (1250, 32), jnp.float32)
        tbl_6 = 0.05 * jax.random.normal(jax.random.fold_in(_tk, 500 + 6), (12500, 32), jnp.float32)
        tbl_7 = 0.05 * jax.random.normal(jax.random.fold_in(_tk, 500 + 7), (12500, 32), jnp.float32)
        tbl_8 = 0.05 * jax.random.normal(jax.random.fold_in(_tk, 500 + 8), (12500, 32), jnp.float32)
        tbl_9 = 0.05 * jax.random.normal(jax.random.fold_in(_tk, 500 + 9), (125000, 32), jnp.float32)
        tbl_10 = 0.05 * jax.random.normal(jax.random.fold_in(_tk, 500 + 10), (125000, 32), jnp.float32)
        tbl_11 = 0.05 * jax.random.normal(jax.random.fold_in(_tk, 500 + 11), (12500, 32), jnp.float32)
        tbl_12 = 0.05 * jax.random.normal(jax.random.fold_in(_tk, 500 + 12), (12500, 32), jnp.float32)
        tbl_13 = 0.05 * jax.random.normal(jax.random.fold_in(_tk, 500 + 13), (125000, 32), jnp.float32)
        tbl_14 = 0.05 * jax.random.normal(jax.random.fold_in(_tk, 500 + 14), (1250, 32), jnp.float32)
        tbl_15 = 0.05 * jax.random.normal(jax.random.fold_in(_tk, 500 + 15), (1250, 32), jnp.float32)
        tbl_16 = 0.05 * jax.random.normal(jax.random.fold_in(_tk, 500 + 16), (1250, 32), jnp.float32)
        tbl_17 = 0.05 * jax.random.normal(jax.random.fold_in(_tk, 500 + 17), (12500, 32), jnp.float32)
        tbl_18 = 0.05 * jax.random.normal(jax.random.fold_in(_tk, 500 + 18), (1000, 32), jnp.float32)
        tbl_19 = 0.05 * jax.random.normal(jax.random.fold_in(_tk, 500 + 19), (1000, 32), jnp.float32)
        tbl_20 = 0.05 * jax.random.normal(jax.random.fold_in(_tk, 500 + 20), (1000, 32), jnp.float32)
        tbl_21 = 0.05 * jax.random.normal(jax.random.fold_in(_tk, 500 + 21), (1000, 32), jnp.float32)
        tbl_22 = 0.05 * jax.random.normal(jax.random.fold_in(_tk, 500 + 22), (12500, 32), jnp.float32)
        tbl_23 = 0.05 * jax.random.normal(jax.random.fold_in(_tk, 500 + 23), (1250, 32), jnp.float32)
        tbl_24 = 0.05 * jax.random.normal(jax.random.fold_in(_tk, 500 + 24), (12500, 32), jnp.float32)
        tbl_25 = 0.05 * jax.random.normal(jax.random.fold_in(_tk, 500 + 25), (1000, 32), jnp.float32)
        tbl_26 = 0.05 * jax.random.normal(jax.random.fold_in(_tk, 500 + 26), (1000, 32), jnp.float32)
        tbl_27 = 0.05 * jax.random.normal(jax.random.fold_in(_tk, 500 + 27), (12500, 32), jnp.float32)
        tbl_28 = 0.05 * jax.random.normal(jax.random.fold_in(_tk, 500 + 28), (1000, 32), jnp.float32)
        tbl_29 = 0.05 * jax.random.normal(jax.random.fold_in(_tk, 500 + 29), (1000, 32), jnp.float32)
        tbl_30 = 0.05 * jax.random.normal(jax.random.fold_in(_tk, 500 + 30), (1250, 32), jnp.float32)
        tbl_31 = 0.05 * jax.random.normal(jax.random.fold_in(_tk, 500 + 31), (125000, 32), jnp.float32)
        tbl_32 = 0.05 * jax.random.normal(jax.random.fold_in(_tk, 500 + 32), (12500, 32), jnp.float32)
        tbl_33 = 0.05 * jax.random.normal(jax.random.fold_in(_tk, 500 + 33), (12500, 32), jnp.float32)
        tbl_34 = 0.05 * jax.random.normal(jax.random.fold_in(_tk, 500 + 34), (12500, 32), jnp.float32)
        tbl_35 = 0.05 * jax.random.normal(jax.random.fold_in(_tk, 500 + 35), (1250, 32), jnp.float32)
        tbl_36 = 0.05 * jax.random.normal(jax.random.fold_in(_tk, 500 + 36), (1000, 32), jnp.float32)
        tbl_37 = 0.05 * jax.random.normal(jax.random.fold_in(_tk, 500 + 37), (1250, 32), jnp.float32)
        tbl_38 = 0.05 * jax.random.normal(jax.random.fold_in(_tk, 500 + 38), (1000, 32), jnp.float32)
        tbl_39 = 0.05 * jax.random.normal(jax.random.fold_in(_tk, 500 + 39), (1000, 32), jnp.float32)
        _rk = jax.random.fold_in(_tk, 7)
        W_top1 = 0.0354441 * jax.random.normal(jax.random.fold_in(_tk, 801), (796, 512), jnp.float32)
        W_top2 = 0.0441942 * jax.random.normal(jax.random.fold_in(_tk, 802), (512, 256), jnp.float32)
        W_top3 = 0.0625 * jax.random.normal(jax.random.fold_in(_tk, 803), (256, 1), jnp.float32)
        b_top1 = jnp.zeros((512,), jnp.float32)
        b_top2 = jnp.zeros((256,), jnp.float32)
        return (dense_ctx, ids, tbl_0, tbl_1, tbl_2, tbl_3, tbl_4, tbl_5, tbl_6, tbl_7, tbl_8, tbl_9, tbl_10, tbl_11, tbl_12, tbl_13, tbl_14, tbl_15, tbl_16, tbl_17, tbl_18, tbl_19, tbl_20, tbl_21, tbl_22, tbl_23, tbl_24, tbl_25, tbl_26, tbl_27, tbl_28, tbl_29, tbl_30, tbl_31, tbl_32, tbl_33, tbl_34, tbl_35, tbl_36, tbl_37, tbl_38, tbl_39, W_top1, b_top1, W_top2, b_top2, W_top3)
    dense_ctx, ids, tbl_0, tbl_1, tbl_2, tbl_3, tbl_4, tbl_5, tbl_6, tbl_7, tbl_8, tbl_9, tbl_10, tbl_11, tbl_12, tbl_13, tbl_14, tbl_15, tbl_16, tbl_17, tbl_18, tbl_19, tbl_20, tbl_21, tbl_22, tbl_23, tbl_24, tbl_25, tbl_26, tbl_27, tbl_28, tbl_29, tbl_30, tbl_31, tbl_32, tbl_33, tbl_34, tbl_35, tbl_36, tbl_37, tbl_38, tbl_39, W_top1, b_top1, W_top2, b_top2, W_top3 = _rec_inputs()

    def _L0_rec_setup():
        import jax, jax.numpy as jnp
        import numpy as np
        NUM_FIELDS = 40
        EMBED_DIM = 32
        BATCH = 512
        NUM_PAIRS = NUM_FIELDS * (NUM_FIELDS - 1) // 2
        key = jax.random.key(seed)
        k1, k2 = jax.random.split(key)
        inputs = jax.random.normal(k1, (BATCH, NUM_FIELDS, EMBED_DIM), dtype=jnp.float32)
        std = (2.0 / (EMBED_DIM + EMBED_DIM)) ** 0.5
        bilinear_matrices = jax.random.normal(k2, (NUM_PAIRS, EMBED_DIM, EMBED_DIM), dtype=jnp.float32) * std
        return {'inputs': inputs, 'bilinear_matrices': bilinear_matrices}
    _L0_rec_all = _L0_rec_setup()
    _L0_rec_in = {k: v for k, v in _L0_rec_all.items() if k in ('bilinear_matrices',)}
    del _L0_rec_all
    return {'dense_ctx': dense_ctx, 'ids': ids, 'tbl_0': tbl_0, 'tbl_1': tbl_1, 'tbl_2': tbl_2, 'tbl_3': tbl_3, 'tbl_4': tbl_4, 'tbl_5': tbl_5, 'tbl_6': tbl_6, 'tbl_7': tbl_7, 'tbl_8': tbl_8, 'tbl_9': tbl_9, 'tbl_10': tbl_10, 'tbl_11': tbl_11, 'tbl_12': tbl_12, 'tbl_13': tbl_13, 'tbl_14': tbl_14, 'tbl_15': tbl_15, 'tbl_16': tbl_16, 'tbl_17': tbl_17, 'tbl_18': tbl_18, 'tbl_19': tbl_19, 'tbl_20': tbl_20, 'tbl_21': tbl_21, 'tbl_22': tbl_22, 'tbl_23': tbl_23, 'tbl_24': tbl_24, 'tbl_25': tbl_25, 'tbl_26': tbl_26, 'tbl_27': tbl_27, 'tbl_28': tbl_28, 'tbl_29': tbl_29, 'tbl_30': tbl_30, 'tbl_31': tbl_31, 'tbl_32': tbl_32, 'tbl_33': tbl_33, 'tbl_34': tbl_34, 'tbl_35': tbl_35, 'tbl_36': tbl_36, 'tbl_37': tbl_37, 'tbl_38': tbl_38, 'tbl_39': tbl_39, 'W_top1': W_top1, 'b_top1': b_top1, 'W_top2': W_top2, 'b_top2': b_top2, 'W_top3': W_top3, 'L0_rec_bilinear_matrices': _L0_rec_in['bilinear_matrices']}

def reference(dense_ctx, ids, tbl_0, tbl_1, tbl_2, tbl_3, tbl_4, tbl_5, tbl_6, tbl_7, tbl_8, tbl_9, tbl_10, tbl_11, tbl_12, tbl_13, tbl_14, tbl_15, tbl_16, tbl_17, tbl_18, tbl_19, tbl_20, tbl_21, tbl_22, tbl_23, tbl_24, tbl_25, tbl_26, tbl_27, tbl_28, tbl_29, tbl_30, tbl_31, tbl_32, tbl_33, tbl_34, tbl_35, tbl_36, tbl_37, tbl_38, tbl_39, W_top1, b_top1, W_top2, b_top2, W_top3, L0_rec_bilinear_matrices):
    import jax
    import jax.numpy as jnp

    def _L0_rec_ref(inputs, bilinear_matrices):
        import jax, jax.numpy as jnp
        import numpy as np
        NUM_FIELDS = 40
        EMBED_DIM = 32
        BATCH = 512
        NUM_PAIRS = NUM_FIELDS * (NUM_FIELDS - 1) // 2
        num_fields = inputs.shape[1]
        iidx, jidx = jnp.triu_indices(num_fields, k=1)
        xi = inputs[:, iidx, :]
        xj = inputs[:, jidx, :]
        out = jnp.einsum('bpd,pde,bpe->bp', xi, bilinear_matrices, xj)
        return out
    e = jnp.stack([tbl_0[ids[:, 0]], tbl_1[ids[:, 1]], tbl_2[ids[:, 2]], tbl_3[ids[:, 3]], tbl_4[ids[:, 4]], tbl_5[ids[:, 5]], tbl_6[ids[:, 6]], tbl_7[ids[:, 7]], tbl_8[ids[:, 8]], tbl_9[ids[:, 9]], tbl_10[ids[:, 10]], tbl_11[ids[:, 11]], tbl_12[ids[:, 12]], tbl_13[ids[:, 13]], tbl_14[ids[:, 14]], tbl_15[ids[:, 15]], tbl_16[ids[:, 16]], tbl_17[ids[:, 17]], tbl_18[ids[:, 18]], tbl_19[ids[:, 19]], tbl_20[ids[:, 20]], tbl_21[ids[:, 21]], tbl_22[ids[:, 22]], tbl_23[ids[:, 23]], tbl_24[ids[:, 24]], tbl_25[ids[:, 25]], tbl_26[ids[:, 26]], tbl_27[ids[:, 27]], tbl_28[ids[:, 28]], tbl_29[ids[:, 29]], tbl_30[ids[:, 30]], tbl_31[ids[:, 31]], tbl_32[ids[:, 32]], tbl_33[ids[:, 33]], tbl_34[ids[:, 34]], tbl_35[ids[:, 35]], tbl_36[ids[:, 36]], tbl_37[ids[:, 37]], tbl_38[ids[:, 38]], tbl_39[ids[:, 39]]], axis=1)
    z = _L0_rec_ref(e, L0_rec_bilinear_matrices)
    z = z.reshape(z.shape[0], -1)
    h = jnp.concatenate([z, dense_ctx], axis=1)
    h = jnp.maximum(h @ W_top1 + b_top1, 0.0)
    h = jnp.maximum(h @ W_top2 + b_top2, 0.0)
    y = h @ W_top3
    return y

_drawn_inputs = setup_inputs


def setup_inputs(seed=0):
    import zlib

    import numpy as np

    out = dict(_drawn_inputs(seed))
    spreads = {'b_top1': (0.0, 0.1), 'b_top2': (0.0, 0.1)}
    factors = {'tbl_0': 3.553,
     'tbl_1': 3.279,
     'tbl_2': 3.424,
     'tbl_3': 3.021,
     'tbl_4': 3.461,
     'tbl_5': 2.947,
     'tbl_6': 3.341,
     'tbl_7': 3.22,
     'tbl_8': 3.067,
     'tbl_9': 2.956,
     'tbl_10': 3.177,
     'tbl_11': 3.713,
     'tbl_13': 3.295,
     'tbl_14': 3.106,
     'tbl_15': 3.214,
     'tbl_16': 3.177,
     'tbl_17': 3.263,
     'tbl_18': 3.371,
     'tbl_19': 3.223,
     'tbl_20': 3.033,
     'tbl_21': 3.234,
     'tbl_22': 3.208,
     'tbl_23': 3.043,
     'tbl_24': 3.176,
     'tbl_25': 3.272,
     'tbl_26': 3.156,
     'tbl_27': 3.375,
     'tbl_28': 3.028,
     'tbl_29': 3.312,
     'tbl_30': 3.246,
     'tbl_31': 2.971,
     'tbl_32': 3.338,
     'tbl_33': 3.026,
     'tbl_34': 3.001,
     'tbl_35': 3.123,
     'tbl_36': 3.479,
     'tbl_37': 3.241,
     'tbl_38': 3.306,
     'tbl_39': 3.058}
    for name, (base, spread) in spreads.items():
        noise = np.random.default_rng([zlib.crc32(name.encode()), seed]).standard_normal(out[name].shape)
        drawn = base * np.exp(spread * noise) if base else spread * noise
        out[name] = jnp.asarray(drawn.astype(out[name].dtype))
    for name, factor in factors.items():
        out[name] = (out[name] * factor).astype(out[name].dtype)
    return out
```

```python
from contextlib import ExitStack

import numpy as np

import concourse.bass as bass
from concourse import mybir

F32 = mybir.dt.float32
F32R = mybir.dt.float32r
I32 = mybir.dt.int32
ALU = mybir.AluOpType
ACT = mybir.ActivationFunctionType

P = 128
H = P // 2
BATCH, FIELDS, DIM = 512, 40, 32
DENSE = 16
HID1, HID2 = 512, 256
BT = BATCH // P
CH = P // DIM
CHUNKS = FIELDS // CH
QUADS = CHUNKS * (CHUNKS + 1) // 2
QZ = DIM // CH
ZC = -(-QUADS // QZ)
NB1, NB2 = HID1 // P, HID2 // P
PIECES = -(-QUADS // CH)
TCOLS = CH * DIM
QCOLS = CH * TCOLS
FIELD_ORDER = list(range(FIELDS))

GATHER_SLOTS, SPLIT_SLOTS, EMB_SLOTS = 3, 2, 2
PROD_SLOTS = 3
STACK_SLOTS = 4
RAW_SLOTS = 2
STEPS = 1 + CH // 2
LEAD = [0, 0, 0, 0, 0, 0, 0, 0, 1, 4]
assert QUADS % QZ != 0 and (QZ - 1) * CH == DIM - CH


def first_quad(c):
    return c * (c + 1) // 2


def steps_done(c, s):
    return STEPS * c + s + 1


def tiles_of(c, r):
    return min(CH, CH * c + CH - 1 - CH * r)


def walk():
    order = [("turn", 0)]
    for c in range(CHUNKS):
        for r in range(c + 1):
            if c + 1 < CHUNKS and r == c + 1 - LEAD[c + 1]:
                order.append(("turn", c + 1))
            order.append(("quad", c, r))
        if c + 1 < CHUNKS and LEAD[c + 1] == 0:
            order.append(("turn", c + 1))
    return order


def build(nc, ids, tables, m_raw, w1, b1, w2, b2, w3, dense_t, ident, sel_z, sel_dense, out):
    order = walk()
    with ExitStack() as ctx:
        def sb(name, shape, dt=F32):
            return ctx.enter_context(nc.sbuf_tensor(name, shape, dt))

        def sem(name):
            return ctx.enter_context(nc.semaphore(name))

        ids_sb = sb("ids_sb", [P, BT * FIELDS], I32)
        gathered = sb("gathered", [P, GATHER_SLOTS, BT, CH * DIM])
        split = sb("split", [P, SPLIT_SLOTS, BT, CH, 2, DIM], F32R)
        emb_t = sb("emb_t", [P, EMB_SLOTS, BATCH])
        x_stack = sb("x_stack", [P, FIELDS - 1, BATCH], F32R)
        raw = sb("raw", [P, RAW_SLOTS, QCOLS])
        m_hi = sb("m_hi", [P, RAW_SLOTS, QCOLS], F32R)
        m_lo = sb("m_lo", [P, RAW_SLOTS, QCOLS], F32R)
        m_stack = sb("m_stack", [P, STACK_SLOTS, CH, QCOLS], F32R)
        prod = sb("prod", [P, PROD_SLOTS, CH, BATCH])
        z_sb = sb("z_sb", [P, ZC, BATCH])
        w1_sb = sb("w1_sb", [P, ZC, HID1])
        w2_sb = sb("w2_sb", [P, NB1, HID2])
        w3_sb = sb("w3_sb", [P, NB2])
        b1_sb = sb("b1_sb", [P, NB1])
        b2_sb = sb("b2_sb", [P, NB2])
        dense_sb = sb("dense_sb", [P, BATCH])
        ident_sb = sb("ident_sb", [P, P])
        ident_r = sb("ident_r", [P, P], F32R)
        sel_z_sb = sb("sel_z_sb", [P, 2 * DIM - CH])
        sel_dense_sb = sb("sel_dense_sb", [P, CH, DIM])
        y_sb = sb("y_sb", [1, BATCH])
        h1_sb = prod[:, (QUADS - 3) % PROD_SLOTS, :, :]
        h2_sb = prod[:, (QUADS - 2) % PROD_SLOTS, 0:NB2, :]

        y_ps = [ctx.enter_context(nc.psum_tensor(f"y_ps{h}", [P, 2, BATCH], F32)) for h in range(2)]
        z_ps = ctx.enter_context(nc.psum_tensor("z_ps", [P, BATCH], F32))
        turn_ps = ctx.enter_context(nc.psum_tensor("turn_ps", [P, BATCH], F32))
        h1a_ps = ctx.enter_context(nc.psum_tensor("h1a_ps", [P, 2, BATCH], F32))
        h1_ps = [h1a_ps[:, 0, :], h1a_ps[:, 1, :], turn_ps[:, :], y_ps[1][:, 1, :]]
        h2_ps = [y_ps[0][:, 0, :], y_ps[0][:, 1, :]]

        ids_landed = sem("ids_landed")
        ident_landed = sem("ident_landed")
        sel_landed = sem("sel_landed")
        w1_landed = sem("w1_landed")
        tail_landed = sem("tail_landed")
        dense_zeroed = sem("dense_zeroed")
        dense_landed = sem("dense_landed")
        rows_landed = [sem(f"rows_landed{c}") for c in range(CHUNKS)]
        raw_landed = [sem(f"raw_landed{s}") for s in range(RAW_SLOTS)]
        stack_landed = [sem(f"stack_landed{s}") for s in range(STACK_SLOTS)]
        ident_rounded = sem("ident_rounded")
        rows_hi = sem("rows_hi")
        rows_lo = sem("rows_lo")
        m_hi_done = sem("m_hi_done")
        m_lo_done = sem("m_lo_done")
        turned = sem("turned")
        copied = sem("copied")
        y_ready = sem("y_ready")
        prod_ready = sem("prod_ready")
        quad_summed = sem("quad_summed")
        z_copied = sem("z_copied")
        h1_ready = sem("h1_ready")
        relu1_act, relu1_dve = sem("relu1_act"), sem("relu1_dve")
        h2_ready = sem("h2_ready")
        relu2_act, relu2_dve = sem("relu2_act"), sem("relu2_dve")
        logit_ready = sem("logit_ready")
        logit_copied = sem("logit_copied")
        out_written = sem("out_written")

        ROWS_INC = 16 * CH * BT
        STACK_INC = 16 * CH * 4

        block = ctx.enter_context(nc.Block())

        @block.sync
        def _(sp):
            def load_raw(k):
                sp.dma_start(raw[:, k % RAW_SLOTS, :], m_raw[:, k, :]).then_inc(raw_landed[k % RAW_SLOTS], 16)

            sp.dma_start(ids_sb[:, :], ids.rearrange("(t p) f -> p t f", p=P)).then_inc(ids_landed, 16)
            load_raw(0)
            sp.dma_start(ident_sb[:, :], ident).then_inc(ident_landed, 16)
            load_raw(1)
            sp.dma_start(sel_z_sb[:, :], sel_z).then_inc(sel_landed, 16)
            sp.dma_start(sel_dense_sb[:, :, :], sel_dense).then_inc(sel_landed, 16)
            for k in range(PIECES):
                sp.wait_ge(m_lo_done, k + 1)
                if k >= STACK_SLOTS:
                    sp.wait_ge(y_ready, 2 * CH * (k - STACK_SLOTS + 1))
                for s in range(CH):
                    src = slice(DIM * s, DIM * s + DIM)
                    for copy in range(4):
                        part = (m_hi, m_hi, m_lo, m_lo)[copy]
                        sp.dma_start(m_stack[DIM * copy:DIM * copy + DIM, k % STACK_SLOTS, s, :].bitcast(F32),
                                     part[src, k % RAW_SLOTS, :].bitcast(F32)
                                     ).then_inc(stack_landed[k % STACK_SLOTS], 16)
                if k + RAW_SLOTS < PIECES:
                    load_raw(k + RAW_SLOTS)
                if k == 0:
                    sp.dma_start(w1_sb[:, :, :], w1.rearrange("(c p) n -> p c n", p=P)).then_inc(w1_landed, 16)
                    sp.wait_ge(dense_zeroed, 1)
                    for s in range(CH):
                        sp.dma_start(dense_sb[DIM * s:DIM * s + CH, :], dense_t[s]).then_inc(dense_landed, 16)
                    sp.dma_start(w2_sb[:, :, :], w2.rearrange("(c p) n -> p c n", p=P)).then_inc(tail_landed, 16)
                    sp.dma_start(w3_sb[:, :], w3).then_inc(tail_landed, 16)
                    sp.dma_start(b1_sb[:, :], b1).then_inc(tail_landed, 16)
                    sp.dma_start(b2_sb[:, :], b2).then_inc(tail_landed, 16)
            sp.wait_ge(logit_copied, 1)
            sp.dma_start(out.rearrange("(a b) o -> a (b o)", a=1), y_sb[:, :]).then_inc(out_written, 16)
            sp.wait_ge(out_written, 16)

        @block.gpsimd
        def _(pool):
            pool.memset(dense_sb[:, :], 0.0).then_inc(dense_zeroed, 1)
            pool.wait_ge(ids_landed, 16)
            for c in range(CHUNKS):
                if c >= GATHER_SLOTS:
                    pool.wait_ge(turned, steps_done(c - GATHER_SLOTS, 0))
                    pool.wait_ge(rows_lo, c - GATHER_SLOTS + 1)
                for j in range(CH):
                    f = FIELD_ORDER[CH * c + j]
                    for t in range(BT):
                        pool.indirect_dma_start(
                            out=gathered[:, c % GATHER_SLOTS, t, DIM * j:DIM * j + DIM], out_offset=None,
                            in_=tables[f][:, :],
                            in_offset=bass.IndirectOffsetOnAxis(
                                ap=ids_sb[:, FIELDS * t + f:FIELDS * t + f + 1], axis=0),
                        ).then_inc(rows_landed[c], 16)

        @block.scalar
        def _(act):
            act.wait_ge(ident_landed, 16)
            nc.scalar.copy(ident_r[:, :], ident_sb[:, :]).then_inc(ident_rounded, 1)

            def m_part(k):
                act.wait_ge(raw_landed[k % RAW_SLOTS], 16 * (k // RAW_SLOTS + 1))
                if k >= RAW_SLOTS:
                    j = k - RAW_SLOTS
                    act.wait_ge(stack_landed[j % STACK_SLOTS], STACK_INC * (j // STACK_SLOTS + 1))
                nc.scalar.copy(m_hi[:, k % RAW_SLOTS, :], raw[:, k % RAW_SLOTS, :]).then_inc(m_hi_done, 1)

            def turn(c):
                act.wait_ge(rows_landed[c], ROWS_INC)
                if c >= SPLIT_SLOTS:
                    act.wait_ge(turned, STEPS * (c - SPLIT_SLOTS + 1))
                nc.scalar.copy(split[:, c % SPLIT_SLOTS, :, :, 0, :],
                               gathered[:, c % GATHER_SLOTS, :, :].rearrange("p t (j d) -> p t j d", d=DIM)
                               ).then_inc(rows_hi, 1)
                act.wait_ge(turned, steps_done(c, 0))
                if c >= EMB_SLOTS:
                    act.wait_ge(prod_ready, 2 * first_quad(c - EMB_SLOTS + 1))
                nc.scalar.copy(emb_t[:, c % EMB_SLOTS, :], turn_ps[:, :]).then_inc(copied, 1)
                for s in range(CH // 2):
                    act.wait_ge(turned, steps_done(c, 1 + s))
                    for j in range(2 * s, min(2 * s + 2, FIELDS - 1 - CH * c)):
                        parts = turn_ps[H * (j % 2):H * (j % 2) + H, :]
                        for copy in range(2):
                            last = nc.scalar.copy(x_stack[H * copy:H * copy + H, CH * c + j, :], parts)
                    last.then_inc(copied, 1)

            for k in range(STACK_SLOTS - 1):
                m_part(k)
            m = 0
            for what in order:
                if what[0] == "turn":
                    turn(what[1])
                    continue
                if m % CH == 0 and m // CH + STACK_SLOTS - 1 < PIECES:
                    m_part(m // CH + STACK_SLOTS - 1)
                if m % QZ == 1 and m > QZ:
                    act.wait_ge(quad_summed, m - 1)
                    nc.scalar.copy(z_sb[:, m // QZ - 1, :], z_ps[:, :]).then_inc(z_copied, 1)
                m += 1
            act.wait_ge(quad_summed, QUADS)
            nc.scalar.copy(z_sb[:, ZC - 1, :], z_ps[:, :]).then_inc(z_copied, 1)
            act.wait_ge(tail_landed, 16 * 4)
            for n in range(0, NB1, 2):
                act.wait_ge(h1_ready, n + 1)
                nc.scalar.activation(h1_sb[:, n, :], h1_ps[n], ACT.Relu, bias=b1_sb[:, n:n + 1]).then_inc(relu1_act, 1)
            act.wait_ge(h2_ready, 1)
            nc.scalar.activation(h2_sb[:, 0, :], h2_ps[0], ACT.Relu, bias=b2_sb[:, 0:1]).then_inc(relu2_act, 1)
            act.wait_ge(logit_ready, 1)
            nc.scalar.copy(y_sb[:, :], z_ps[0:1, :]).then_inc(logit_copied, 1)

        @block.vector
        def _(dve):
            def m_part(k):
                dve.wait_ge(m_hi_done, k + 1)
                nc.vector.tensor_tensor(m_lo[:, k % RAW_SLOTS, :], raw[:, k % RAW_SLOTS, :],
                                        m_hi[:, k % RAW_SLOTS, :].bitcast(F32), ALU.subtract).then_inc(m_lo_done, 1)

            def turn(c):
                dve.wait_ge(rows_hi, c + 1)
                nc.vector.tensor_tensor(split[:, c % SPLIT_SLOTS, :, :, 1, :],
                                        gathered[:, c % GATHER_SLOTS, :, :].rearrange("p t (j d) -> p t j d", d=DIM),
                                        split[:, c % SPLIT_SLOTS, :, :, 0, :].bitcast(F32),
                                        ALU.subtract).then_inc(rows_lo, 1)

            for k in range(STACK_SLOTS - 1):
                m_part(k)
            m = 0
            for what in order:
                if what[0] == "turn":
                    turn(what[1])
                    continue
                c, r = what[1:]
                if m % CH == 0 and m // CH + STACK_SLOTS - 1 < PIECES:
                    m_part(m // CH + STACK_SLOTS - 1)
                if r == 0:
                    dve.wait_ge(copied, steps_done(c, 0))
                for h in range(2):
                    n = min(2, tiles_of(c, r) - 2 * h)
                    if h == 0 and m >= PROD_SLOTS:
                        dve.wait_ge(quad_summed, m - PROD_SLOTS + 1)
                    dve.wait_ge(y_ready, 2 * m + h + 1)
                    nc.vector.tensor_tensor(prod[:, m % PROD_SLOTS, 2 * h:2 * h + n, :], y_ps[h][:, 0:n, :],
                                            emb_t[:, c % EMB_SLOTS:c % EMB_SLOTS + 1, :].broadcast_to([P, n, BATCH]),
                                            ALU.mult).then_inc(prod_ready, 1)
                m += 1
            dve.wait_ge(tail_landed, 16 * 4)
            for n in range(1, NB1, 2):
                dve.wait_ge(h1_ready, n + 1)
                nc.vector.tensor_scalar(h1_sb[:, n, :], h1_ps[n], b1_sb[:, n:n + 1], 0.0, ALU.add,
                                        ALU.max).then_inc(relu1_dve, 1)
            dve.wait_ge(h2_ready, 2)
            nc.vector.tensor_scalar(h2_sb[:, 1, :], h2_ps[1], b2_sb[:, 1:2], 0.0, ALU.add,
                                    ALU.max).then_inc(relu2_dve, 1)

        @block.tensor
        def _(pe):
            def turn_step(c, s):
                n = steps_done(c, s) - 1
                if n:
                    pe.wait_ge(copied, n)
                if s == 0:
                    pe.wait_ge(rows_landed[c], ROWS_INC)
                if s == 1:
                    pe.wait_ge(rows_lo, c + 1)
                for t in range(BT):
                    cols = turn_ps[:, P * t:P * t + P]
                    if s == 0:
                        mm = nc.tensor.matmul(cols, gathered[:, c % GATHER_SLOTS, t, :], ident_sb[:, :],
                                              start=True, stop=True)
                    else:
                        rows = split[:, c % SPLIT_SLOTS, t, 2 * s - 2:2 * s, :, :].rearrange("p j h d -> p (j h d)")
                        mm = nc.tensor.matmul(cols, rows, ident_r[:, :], start=True, stop=True)
                mm.then_inc(turned, 1)

            def turn(c):
                for s in range(STEPS):
                    turn_step(c, s)

            def bilinear(m, c, r, h):
                k = m // CH
                if h == 0 and m % CH == 0:
                    pe.wait_ge(stack_landed[k % STACK_SLOTS], STACK_INC * (k // STACK_SLOTS + 1))
                if h == 0 and r == c:
                    pe.wait_ge(copied, STEPS * (c + 1))
                if m:
                    pe.wait_ge(prod_ready, 2 * (m - 1) + h + 1)
                for t in range(2 * h, min(2 * h + 2, tiles_of(c, r))):
                    mm = nc.tensor.matmul(y_ps[h][:, t - 2 * h, :],
                                          m_stack[:, k % STACK_SLOTS, m % CH, TCOLS * t:TCOLS * t + TCOLS],
                                          x_stack[:, CH * r + t, :], start=True, stop=True)
                mm.then_inc(y_ready, 1)

            def sum_quad(m, tiles):
                k = m % QZ
                if k == 0 and m:
                    pe.wait_ge(z_copied, m // QZ)
                if m == QZ * (ZC - 1):
                    pe.wait_ge(dense_landed, 16 * CH)
                    for q in range(CH):
                        nc.tensor.matmul(z_ps[DIM * q:DIM * q + DIM, :], sel_dense_sb[:, q, :], dense_sb[:, :],
                                         start=True, stop=False)
                pe.wait_ge(prod_ready, 2 * m + 2)
                for t in range(tiles):
                    first = m < QZ * (ZC - 1) and (k == 0 or (m == 1 and t == CH - 1))
                    last = k == QZ - 1 or m == QUADS - 1 or (m == QUADS - 2 and t == CH - 1)
                    mm = nc.tensor.matmul(z_ps[DIM * t:DIM * t + DIM, :],
                                          sel_z_sb[:, CH * (QZ - 1 - k):CH * (QZ - 1 - k) + DIM],
                                          prod[:, m % PROD_SLOTS, t, :], start=first,
                                          stop=last)
                mm.then_inc(quad_summed, 1)

            def hidden1(zc, n):
                pe.wait_ge(z_copied, zc + 1)
                mm = nc.tensor.matmul(h1_ps[n], w1_sb[:, zc, P * n:P * n + P], z_sb[:, zc, :],
                                      start=(zc == 0), stop=(zc == ZC - 1))
                if zc == ZC - 1:
                    mm.then_inc(h1_ready, 1)

            pe.wait_ge(ident_landed, 16)
            pe.wait_ge(ident_rounded, 1)
            last_turn = max(n for n, what in enumerate(order) if what[0] == "turn")
            todo2 = list(range(ZC - 1))
            m = 0
            before = None
            for n, what in enumerate(order):
                if what[0] == "turn":
                    if before is not None and what[1] < CHUNKS - 2:
                        if before[0] == 0:
                            pe.wait_ge(sel_landed, 32)
                        sum_quad(*before)
                        before = None
                    turn(what[1])
                    continue
                c, r = what[1:]
                bilinear(m, c, r, 0)
                if before is not None:
                    if before[0] == 0:
                        pe.wait_ge(sel_landed, 32)
                    sum_quad(*before)
                bilinear(m, c, r, 1)
                before = (m, tiles_of(c, r))
                if m % QZ == 2 and m > QZ:
                    if m // QZ == 1:
                        pe.wait_ge(w1_landed, 16)
                    hidden1(m // QZ - 1, 0)
                    hidden1(m // QZ - 1, 1)
                if n > last_turn and c == CHUNKS - 1 and todo2 and QZ * (todo2[0] + 1) + 1 < m:
                    if todo2[0] == 0:
                        pe.wait_ge(copied, STEPS * CHUNKS)
                    hidden1(todo2.pop(0), 2)
                m += 1
            pe.wait_ge(prod_ready, 2 * (QUADS - 1))
            for zc in range(2):
                hidden1(zc, 3)
            sum_quad(*before)
            for zc in todo2:
                hidden1(zc, 2)
            for zc in range(2, ZC - 1):
                hidden1(zc, 3)
            for n in range(NB1):
                hidden1(ZC - 1, n)
            pe.wait_ge(tail_landed, 16 * 4)
            for k in range(NB1):
                pe.wait_ge((relu1_act, relu1_dve)[k % 2], k // 2 + 1)
                for n in range(NB2):
                    mm = nc.tensor.matmul(h2_ps[n], w2_sb[:, k, P * n:P * n + P], h1_sb[:, k, :],
                                          start=(k == 0), stop=(k == NB1 - 1))
                    if k == NB1 - 1:
                        mm.then_inc(h2_ready, 1)
            for n in range(NB2):
                pe.wait_ge((relu2_act, relu2_dve)[n], 1)
                mm = nc.tensor.matmul(z_ps[0:1, :], w3_sb[:, n:n + 1], h2_sb[:, n, :], start=(n == 0), stop=(n == NB2 - 1))
            mm.then_inc(logit_ready, 1)


def layouts(w_top1, dense_ctx, bilinear):
    pair = {}
    for i in range(FIELDS):
        for j in range(i + 1, FIELDS):
            pair[i, j] = len(pair)
    m_raw = np.zeros((CH, DIM, PIECES, CH, CH, DIM), bilinear.dtype)
    w1 = np.zeros((ZC * P, w_top1.shape[1]), w_top1.dtype)
    for c in range(CHUNKS):
        for j in range(CH):
            for i in range(CH * c + j):
                m, t = first_quad(c) + i // CH, i % CH
                a, b = FIELD_ORDER[i], FIELD_ORDER[CH * c + j]
                p = pair[min(a, b), max(a, b)]
                m_raw[m % CH, :, m // CH, t, j] = bilinear[p] if a < b else bilinear[p].T
                w1[P * (m // QZ) + DIM * t + CH * (m % QZ) + j] = w_top1[p]
    for f in range(DENSE):
        w1[P * (ZC - 1) + DIM * (f // CH) + DIM - CH + f % CH] = w_top1[len(pair) + f]
    dense_t = np.ascontiguousarray(dense_ctx.T.reshape(CH, CH, BATCH).transpose(1, 0, 2))
    return m_raw.reshape(P, PIECES, QCOLS), w1, dense_t


def selectors():
    sel_z = np.zeros((P, 2 * DIM - CH), np.float32)
    sel_dense = np.zeros((P, CH, DIM), np.float32)
    for p in range(P):
        sel_z[p, DIM - CH + p // DIM] = 1
    for q in range(CH):
        for s in range(CH):
            sel_dense[DIM * s + q, q, DIM - CH + s] = 1
    return np.eye(P, dtype=np.float32), sel_z, sel_dense


def kernel(**inputs):
    import concourse.bacc as _bacc
    from concourse.bass_utils import run_bass_kernel_spmd as _run

    given = {name: np.asarray(a) for name, a in inputs.items()}
    m_raw, w1, dense_t = layouts(given["W_top1"], given["dense_ctx"], given["L0_rec_bilinear_matrices"])
    ident, sel_z, sel_dense = selectors()
    laid = {"ids": given["ids"]}
    for f in range(FIELDS):
        laid[f"tbl_{f}"] = given[f"tbl_{f}"]
    laid["m_raw"] = m_raw
    laid["w1"] = w1
    laid["b1"] = given["b_top1"].reshape(NB1, P).T
    laid["w2"] = given["W_top2"]
    laid["b2"] = given["b_top2"].reshape(NB2, P).T
    laid["w3"] = given["W_top3"].reshape(NB2, P).T
    laid["dense_t"] = dense_t
    laid["ident"] = ident
    laid["sel_z"] = sel_z
    laid["sel_dense"] = sel_dense

    nc = _bacc.Bacc("TRN2", target_bir_lowering=False, num_devices=1)
    arrays, aps = {}, {}
    for name, a in laid.items():
        a = np.ascontiguousarray(a)
        arrays[f"in_{name}"] = a
        aps[name] = nc.dram_tensor(f"in_{name}", a.shape, mybir.dt.from_np(a.dtype), kind="ExternalInput").ap()
    out = nc.dram_tensor("out_0", (BATCH, 1), F32, kind="ExternalOutput").ap()
    build(nc, aps["ids"], [aps[f"tbl_{f}"] for f in range(FIELDS)], aps["m_raw"], aps["w1"], aps["b1"], aps["w2"],
          aps["b2"], aps["w3"], aps["dense_t"], aps["ident"], aps["sel_z"], aps["sel_dense"], out)
    r = _run(nc, [arrays], core_ids=[0])
    return r.results[0]["out_0"]
```

```python
from contextlib import ExitStack

import numpy as np

import concourse.bass as bass
from concourse import mybir

F32 = mybir.dt.float32
F32R = mybir.dt.float32r
I32 = mybir.dt.int32
ALU = mybir.AluOpType
ACT = mybir.ActivationFunctionType

P = 128
H = P // 2
BATCH, FIELDS, DIM = 512, 40, 32
DENSE = 16
HID1, HID2 = 512, 256
BT = BATCH // P
CH = P // DIM
CHUNKS = FIELDS // CH
QUADS = CHUNKS * (CHUNKS + 1) // 2
QZ = DIM // CH
ZC = -(-QUADS // QZ)
NB1, NB2 = HID1 // P, HID2 // P
BLK = 2
PQ = CH * BLK
PIECES = -(-QUADS // PQ)
TCOLS = CH * DIM
QCOLS = CH * TCOLS
SMALL = 1000
LOOKED = [18, 19, 20, 21, 25, 26, 28, 29]
FIELD_ORDER = LOOKED + [f for f in range(FIELDS) if f not in LOOKED]
LC = len(LOOKED) // CH
KT = -(-SMALL // P)
ONEHOT_SLOTS = 8

GATHER_SLOTS, EMB_SLOTS = 3, 2
PROD_SLOTS = 3
STACK_SLOTS = 2
RAW_SLOTS = 1
PART_SLOTS = 2
STEPS = 1 + CH // 2
LEAD = {2: (2, [2, 1, 0]), 3: (2, [2, 1, 0]), 4: (3, [3, 2, 1]), 5: (4, [3, 2, 1]), 6: (4, [3, 2, 1]),
        7: (5, [4, 3, 1]), 8: (5, [4, 3, 1]), 9: (6, [4, 3, 1])}
Y_SLOTS = 3
AHEAD = 4
AHEAD_AT = [36, 37, 38, 39]
assert QUADS % QZ != 0 and (QZ - 1) * CH == DIM - CH


def first_quad(c):
    return c * (c + 1) // 2


def steps_done(c, s):
    return c + 1 if c < LC else FILLS.index(("turn", c, s)) + LC + 1


def ahead_done(n):
    return FILLS.index(("ahead", n)) + LC + 1


def tiles_of(c, r):
    return min(CH, CH * c + CH - 1 - CH * r)


def walk():
    order = []
    for c in range(CHUNKS):
        for r in range(c + 2):
            left, m = c + 1 - r, first_quad(c) + r
            if LC <= c + 1 < CHUNKS:
                split_at, steps_at = LEAD[c + 1]
                if left == split_at:
                    order.append(("split", c + 1))
                order += [("turn", c + 1, s) for s in range(STEPS) if steps_at[s] == left]
            if left == 0:
                break
            order.append(("quad", m, c, r))
            if m % PQ == PQ - 1 and m // PQ + STACK_SLOTS < PIECES:
                order.append(("piece", m // PQ + STACK_SLOTS))
            if m % QZ == 1 and m > QZ:
                order.append(("z", m // QZ - 1))
            order += [("ahead", n) for n in range(NB1) if AHEAD_AT[n] == m]
    return order


ORDER = walk()
FILLS = [what for what in ORDER if what[0] in ("turn", "ahead")]


def build(nc, ids, ids_rows, small, row_of, tables, m_raw, w1, b1, w2, b2, w3, dense_t, ident, sel_z, sel_dense, sel_emb, out):
    with ExitStack() as ctx:
        def sb(name, shape, dt=F32):
            return ctx.enter_context(nc.sbuf_tensor(name, shape, dt))

        def sem(name):
            return ctx.enter_context(nc.semaphore(name))

        ids_sb = sb("ids_sb", [P, BT * FIELDS], I32)
        gathered = sb("gathered", [P, GATHER_SLOTS, BT, CH * DIM])
        split = sb("split", [P, BT, CH, 2, DIM], F32R)
        emb_t = sb("emb_t", [P, EMB_SLOTS, BATCH])
        x_stack = sb("x_stack", [P, FIELDS - 1, BATCH], F32R)
        raw = sb("raw", [P, RAW_SLOTS, BLK, QCOLS])
        m_hi = sb("m_hi", [P, PART_SLOTS, BLK, QCOLS], F32R)
        m_lo = sb("m_lo", [P, PART_SLOTS, BLK, QCOLS], F32R)
        m_stack = sb("m_stack", [P, STACK_SLOTS, BLK, CH, QCOLS], F32R)
        prod = sb("prod", [P, PROD_SLOTS, CH, BATCH])
        z_sb = sb("z_sb", [P, ZC, BATCH])
        w1_sb = sb("w1_sb", [P, ZC, HID1])
        w2_sb = sb("w2_sb", [P, NB1, HID2])
        w3_sb = sb("w3_sb", [P, NB2])
        b1_sb = sb("b1_sb", [P, NB1])
        b2_sb = sb("b2_sb", [P, NB2])
        dense_sb = sb("dense_sb", [P, BATCH])
        ident_sb = sb("ident_sb", [P, P])
        ident_r = sb("ident_r", [P, P], F32R)
        sel_z_sb = sb("sel_z_sb", [P, 2 * DIM - CH])
        sel_dense_sb = sb("sel_dense_sb", [P, CH, DIM])
        row_of_sb = sb("row_of_sb", [P, KT])
        sel_emb_sb = sb("sel_emb_sb", [P, 2 * P - DIM])
        sel_emb_r = sb("sel_emb_r", [P, 2 * P - DIM], F32R)
        y_sb = emb_t[0:1, CHUNKS % EMB_SLOTS, :]
        looked_ids = prod[:, :, :, :].rearrange("p a b c -> p (a b c)")[:, 0:len(LOOKED) * BATCH].bitcast(I32)
        small_sb = z_sb[:, :, :].rearrange("p a b -> p (a b)")[:, 0:len(LOOKED) * KT * DIM].rearrange(
            "p (f k d) -> p f k d", f=len(LOOKED), k=KT)
        parts_at, onehot_at = 4 * CH, 6 * CH
        small_parts = x_stack[:, parts_at:onehot_at, :].rearrange("p a b -> p (a b)").rearrange(
            "p (f k h d) -> p f k h d", f=len(LOOKED), k=KT, h=2)
        onehot = x_stack[:, onehot_at:onehot_at + ONEHOT_SLOTS, :]
        h1_sb = prod[:, (QUADS - 3) % PROD_SLOTS, :, :]
        h2_sb = prod[:, (QUADS - 2) % PROD_SLOTS, 0:NB2, :]

        y_ps = [ctx.enter_context(nc.psum_tensor(f"y_ps{s}", [P, 2, BATCH], F32)) for s in range(Y_SLOTS)]
        z_ps = ctx.enter_context(nc.psum_tensor("z_ps", [P, BATCH], F32))
        turn_ps = ctx.enter_context(nc.psum_tensor("turn_ps", [P, BATCH], F32))
        look_ps = [y_ps[s][:, b, :] for s in range(Y_SLOTS - 1) for b in range(2)]
        last_half = 2 * QUADS - 1
        late = y_ps[(last_half - 2) % Y_SLOTS]
        h1_ps = [late[:, 0, :], late[:, 1, :], turn_ps[:, :], y_ps[last_half % Y_SLOTS][:, 1, :]]
        h2_ps = [y_ps[(last_half - 1) % Y_SLOTS][:, b, :] for b in range(NB2)]
        h1_ahead = [w1_sb[:, 0:AHEAD, P * n:P * n + P] for n in range(NB1)]

        ids_landed = sem("ids_landed")
        ident_landed = sem("ident_landed")
        sel_landed = sem("sel_landed")
        w1_landed = sem("w1_landed")
        tail_landed = sem("tail_landed")
        dense_zeroed = sem("dense_zeroed")
        dense_landed = sem("dense_landed")
        rows_landed = [sem(f"rows_landed{c}") for c in range(CHUNKS)]
        raw_landed = [sem(f"raw_landed{s}") for s in range(RAW_SLOTS)]
        stack_landed = [sem(f"stack_landed{s}") for s in range(STACK_SLOTS)]
        ids_rows_landed = [sem(f"ids_rows_landed{c}") for c in range(LC)]
        small_landed = sem("small_landed")
        row_of_landed = sem("row_of_landed")
        consts_rounded = sem("consts_rounded")
        small_hi, small_lo = sem("small_hi"), sem("small_lo")
        onehot_ready = sem("onehot_ready")
        onehot_used = sem("onehot_used")
        looked_copied = sem("looked_copied")
        rows_hi = sem("rows_hi")
        rows_lo = sem("rows_lo")
        m_hi_done = sem("m_hi_done")
        m_lo_done = sem("m_lo_done")
        filled = sem("filled")
        emptied = sem("emptied")
        y_ready = sem("y_ready")
        prod_ready = sem("prod_ready")
        quad_summed = sem("quad_summed")
        z_copied = sem("z_copied")
        h1_ready = sem("h1_ready")
        h1_added = sem("h1_added")
        h1_relu = sem("h1_relu")
        h2_ready = sem("h2_ready")
        relu2_act, relu2_dve = sem("relu2_act"), sem("relu2_dve")
        logit_ready = sem("logit_ready")
        logit_copied = sem("logit_copied")
        out_written = sem("out_written")

        ROWS_INC = 16 * CH * BT
        STACK_INC = 16 * CH * 4

        block = ctx.enter_context(nc.Block())

        @block.sync
        def _(sp):
            def load_raw(k):
                sp.dma_start(raw[:, k % RAW_SLOTS, :, :], m_raw[:, BLK * k:BLK * k + BLK, :]).then_inc(raw_landed[k % RAW_SLOTS], 16)

            sp.dma_start(ids_sb[:, :], ids.rearrange("(t p) f -> p t f", p=P)).then_inc(ids_landed, 16)
            load_raw(0)
            sp.dma_start(row_of_sb[:, :], row_of).then_inc(row_of_landed, 16)
            sp.dma_start(small_sb, small).then_inc(small_landed, 16)
            for c in range(LC):
                sp.dma_start(looked_ids[:, CH * BATCH * c:CH * BATCH * (c + 1)],
                             ids_rows[c:c + 1, :].broadcast_to([P, CH * BATCH])).then_inc(ids_rows_landed[c], 16)
            sp.dma_start(ident_sb[:, :], ident).then_inc(ident_landed, 16)
            sp.dma_start(sel_emb_sb[:, :], sel_emb).then_inc(ident_landed, 16)
            sp.dma_start(sel_z_sb[:, :], sel_z).then_inc(sel_landed, 16)
            sp.dma_start(sel_dense_sb[:, :, :], sel_dense).then_inc(sel_landed, 16)
            for k in range(PIECES):
                sp.wait_ge(m_lo_done, k + 1)
                if k + RAW_SLOTS < PIECES:
                    load_raw(k + RAW_SLOTS)
                if k >= STACK_SLOTS:
                    sp.wait_ge(y_ready, 2 * PQ * (k - STACK_SLOTS + 1))
                for s in range(CH):
                    src = slice(DIM * s, DIM * s + DIM)
                    for copy in range(4):
                        part = (m_hi, m_hi, m_lo, m_lo)[copy]
                        sp.dma_start(m_stack[DIM * copy:DIM * copy + DIM, k % STACK_SLOTS, :, s, :].bitcast(F32),
                                     part[src, k % PART_SLOTS, :, :].bitcast(F32)
                                     ).then_inc(stack_landed[k % STACK_SLOTS], 16)
                if k == 0:
                    sp.dma_start(w1_sb[:, :, :], w1.rearrange("(c p) n -> p c n", p=P)).then_inc(w1_landed, 16)
                    sp.wait_ge(dense_zeroed, 1)
                    for s in range(CH):
                        sp.dma_start(dense_sb[DIM * s:DIM * s + CH, :], dense_t[s]).then_inc(dense_landed, 16)
                    sp.dma_start(w2_sb[:, :, :], w2.rearrange("(c p) n -> p c n", p=P)).then_inc(tail_landed, 16)
                    sp.dma_start(w3_sb[:, :], w3).then_inc(tail_landed, 16)
                    sp.dma_start(b1_sb[:, :], b1).then_inc(tail_landed, 16)
                    sp.dma_start(b2_sb[:, :], b2).then_inc(tail_landed, 16)
            sp.wait_ge(logit_copied, 1)
            sp.dma_start(out.rearrange("(a b) o -> a (b o)", a=1), y_sb).then_inc(out_written, 16)
            sp.wait_ge(out_written, 16)

        @block.gpsimd
        def _(pool):
            pool.memset(dense_sb[:, :], 0.0).then_inc(dense_zeroed, 1)
            pool.wait_ge(ids_landed, 16)
            for c in range(LC, CHUNKS):
                if c - LC >= GATHER_SLOTS:
                    pool.wait_ge(filled, steps_done(c - GATHER_SLOTS, 0))
                    pool.wait_ge(rows_lo, c - LC - GATHER_SLOTS + 1)
                for j in range(CH):
                    f = FIELD_ORDER[CH * c + j]
                    for t in range(BT):
                        pool.indirect_dma_start(
                            out=gathered[:, c % GATHER_SLOTS, t, DIM * j:DIM * j + DIM], out_offset=None,
                            in_=tables[f][:, :],
                            in_offset=bass.IndirectOffsetOnAxis(
                                ap=ids_sb[:, FIELDS * t + f:FIELDS * t + f + 1], axis=0),
                        ).then_inc(rows_landed[c], 16)

        @block.scalar
        def _(act):
            def m_part(k):
                act.wait_ge(raw_landed[k % RAW_SLOTS], 16 * (k // RAW_SLOTS + 1))
                if k >= PART_SLOTS:
                    j = k - PART_SLOTS
                    act.wait_ge(stack_landed[j % STACK_SLOTS], STACK_INC * (j // STACK_SLOTS + 1))
                nc.scalar.copy(m_hi[:, k % PART_SLOTS, :, :], raw[:, k % RAW_SLOTS, :, :]).then_inc(m_hi_done, 1)

            def split_rows(c):
                act.wait_ge(rows_landed[c], ROWS_INC)
                if c > LC:
                    act.wait_ge(filled, steps_done(c - 1, STEPS - 1))
                nc.scalar.copy(split[:, :, :, 0, :],
                               gathered[:, c % GATHER_SLOTS, :, :].rearrange("p t (j d) -> p t j d", d=DIM)
                               ).then_inc(rows_hi, 1)

            def copy_emb(c):
                act.wait_ge(filled, steps_done(c, 0))
                if c >= EMB_SLOTS:
                    act.wait_ge(prod_ready, 2 * first_quad(c - EMB_SLOTS + 1))
                nc.scalar.copy(emb_t[:, c % EMB_SLOTS, :], turn_ps[:, :]).then_inc(emptied, 1)

            def copy_stack(i, parts):
                for copy in range(2):
                    last = nc.scalar.copy(x_stack[H * copy:H * copy + H, i, :], parts)
                return last

            m_part(0)
            act.wait_ge(small_landed, 16)
            for f in range(len(LOOKED)):
                nc.scalar.copy(small_parts[:, f, :, 0, :], small_sb[:, f, :, :]).then_inc(small_hi, 1)
            act.wait_ge(ident_landed, 32)
            nc.scalar.copy(ident_r[:, :], ident_sb[:, :]).then_inc(consts_rounded, 1)
            nc.scalar.copy(sel_emb_r[:, :], sel_emb_sb[:, :]).then_inc(consts_rounded, 1)
            m_part(1)
            for c in range(LC):
                for i in range(CH * c, CH * c + CH):
                    act.wait_ge(onehot_used, KT * (i + 1))
                    copy_stack(i, look_ps[i % len(look_ps)][0:H, :]).then_inc(looked_copied, 1)
                copy_emb(c)
            for what, *at in ORDER:
                if what == "split":
                    split_rows(*at)
                elif what == "turn":
                    c, s = at
                    if s == 0:
                        copy_emb(c)
                        continue
                    act.wait_ge(filled, steps_done(c, s))
                    for j in range(2 * s - 2, min(2 * s, FIELDS - 1 - CH * c)):
                        last = copy_stack(CH * c + j, turn_ps[H * (j % 2):H * (j % 2) + H, :])
                    last.then_inc(emptied, 1)
                elif what == "ahead":
                    if at[0] == 0:
                        act.wait_ge(tail_landed, 16 * 4)
                    act.wait_ge(filled, ahead_done(*at))
                    nc.scalar.activation(h1_ahead[at[0]], turn_ps[:, :].rearrange("p (a b) -> p a b", b=P),
                                         ACT.Identity, bias=b1_sb[:, at[0]:at[0] + 1]).then_inc(emptied, 1)
                elif what == "piece":
                    m_part(*at)
                elif what == "z":
                    act.wait_ge(quad_summed, QZ * (at[0] + 1))
                    nc.scalar.copy(z_sb[:, at[0], :], z_ps[:, :]).then_inc(z_copied, 1)
            act.wait_ge(quad_summed, QUADS)
            nc.scalar.copy(z_sb[:, ZC - 1, :], z_ps[:, :]).then_inc(z_copied, 1)
            for n in range(NB1):
                act.wait_ge(h1_added, n + 1)
                nc.scalar.activation(h1_sb[:, n, :], h1_sb[:, n, :], ACT.Relu).then_inc(h1_relu, 1)
            act.wait_ge(h2_ready, 1)
            nc.scalar.activation(h2_sb[:, 0, :], h2_ps[0], ACT.Relu, bias=b2_sb[:, 0:1]).then_inc(relu2_act, 1)
            act.wait_ge(logit_ready, 1)
            nc.scalar.copy(y_sb, z_ps[0:1, :]).then_inc(logit_copied, 1)

        @block.vector
        def _(dve):
            def m_part(k):
                dve.wait_ge(m_hi_done, k + 1)
                nc.vector.tensor_tensor(m_lo[:, k % PART_SLOTS, :, :], raw[:, k % RAW_SLOTS, :, :],
                                        m_hi[:, k % PART_SLOTS, :, :].bitcast(F32), ALU.subtract).then_inc(m_lo_done, 1)

            def split_rows(c):
                dve.wait_ge(rows_hi, c - LC + 1)
                nc.vector.tensor_tensor(split[:, :, :, 1, :],
                                        gathered[:, c % GATHER_SLOTS, :, :].rearrange("p t (j d) -> p t j d", d=DIM),
                                        split[:, :, :, 0, :].bitcast(F32), ALU.subtract).then_inc(rows_lo, 1)

            m_part(0)
            dve.wait_ge(row_of_landed, 16)
            for f in range(len(LOOKED)):
                dve.wait_ge(small_hi, f + 1)
                nc.vector.tensor_tensor(small_parts[:, f, :, 1, :], small_sb[:, f, :, :],
                                        small_parts[:, f, :, 0, :].bitcast(F32), ALU.subtract).then_inc(small_lo, 1)
                if f % CH == 0:
                    dve.wait_ge(ids_rows_landed[f // CH], 16)
                for k in range(KT):
                    n = KT * f + k
                    if n >= ONEHOT_SLOTS:
                        dve.wait_ge(onehot_used, n - ONEHOT_SLOTS + 1)
                    nc.vector.tensor_scalar(onehot[:, n % ONEHOT_SLOTS, :], looked_ids[:, BATCH * f:BATCH * (f + 1)],
                                            row_of_sb[:, k:k + 1], None, ALU.is_equal).then_inc(onehot_ready, 1)
                if f == 0:
                    m_part(1)
            for what, *at in ORDER:
                if what == "split":
                    split_rows(*at)
                elif what == "piece":
                    m_part(*at)
                if what != "quad":
                    continue
                m, c, r = at
                if r == 0:
                    dve.wait_ge(emptied, steps_done(c, 0))
                for h in range(2):
                    n = min(2, tiles_of(c, r) - 2 * h)
                    if h == 0 and m >= PROD_SLOTS:
                        dve.wait_ge(quad_summed, m - PROD_SLOTS + 1)
                    dve.wait_ge(y_ready, 2 * m + h + 1)
                    nc.vector.tensor_tensor(prod[:, m % PROD_SLOTS, 2 * h:2 * h + n, :],
                                            y_ps[(2 * m + h) % Y_SLOTS][:, 0:n, :],
                                            emb_t[:, c % EMB_SLOTS:c % EMB_SLOTS + 1, :].broadcast_to([P, n, BATCH]),
                                            ALU.mult).then_inc(prod_ready, 1)
            dve.wait_ge(emptied, ahead_done(NB1 - 1))
            for n in range(NB1):
                dve.wait_ge(h1_ready, n + 1)
                nc.vector.tensor_tensor(h1_sb[:, n, :].rearrange("p (a b) -> p a b", b=P),
                                        h1_ps[n].rearrange("p (a b) -> p a b", b=P), h1_ahead[n],
                                        ALU.add).then_inc(h1_added, 1)
            dve.wait_ge(h2_ready, 2)
            nc.vector.tensor_scalar(h2_sb[:, 1, :], h2_ps[1], b2_sb[:, 1:2], 0.0, ALU.add,
                                    ALU.max).then_inc(relu2_dve, 1)

        @block.tensor
        def _(pe):
            def turn_step(c, s):
                n = steps_done(c, s) - 1
                if n:
                    pe.wait_ge(emptied, n)
                if s == 0:
                    pe.wait_ge(rows_landed[c], ROWS_INC)
                if s == 1:
                    pe.wait_ge(rows_lo, c - LC + 1)
                for t in range(BT):
                    cols = turn_ps[:, P * t:P * t + P]
                    if s == 0:
                        mm = nc.tensor.matmul(cols, gathered[:, c % GATHER_SLOTS, t, :], ident_sb[:, :],
                                              start=True, stop=True)
                    else:
                        rows = split[:, t, 2 * s - 2:2 * s, :, :].rearrange("p j h d -> p (j h d)")
                        mm = nc.tensor.matmul(cols, rows, ident_r[:, :], start=True, stop=True)
                mm.then_inc(filled, 1)

            def look_up(i):
                if i >= len(look_ps):
                    pe.wait_ge(looked_copied, i - len(look_ps) + 1)
                pe.wait_ge(small_lo, i + 1)
                for k in range(KT):
                    n = KT * i + k
                    pe.wait_ge(onehot_ready, n + 1)
                    mm = nc.tensor.matmul(look_ps[i % len(look_ps)][0:H, :],
                                          small_parts[:, i, k, :, :].rearrange("p h d -> p (h d)"),
                                          onehot[:, n % ONEHOT_SLOTS, :], start=(k == 0), stop=(k == KT - 1))
                    mm.then_inc(onehot_used, 1)

            def turn_looked(c):
                pe.wait_ge(looked_copied, CH * (c + 1))
                if c:
                    pe.wait_ge(emptied, c)
                for j in range(CH):
                    mm = nc.tensor.matmul(turn_ps[:, :], sel_emb_r[:, DIM * (CH - 1 - j):DIM * (CH - 1 - j) + P],
                                          x_stack[:, CH * c + j, :], start=(j == 0), stop=(j == CH - 1))
                mm.then_inc(filled, 1)

            def bilinear(m, c, r, h):
                k = m // PQ
                if h == 0 and m % PQ == 0:
                    pe.wait_ge(stack_landed[k % STACK_SLOTS], STACK_INC * (k // STACK_SLOTS + 1))
                if h == 0 and r == c:
                    pe.wait_ge(emptied, steps_done(c, STEPS - 1))
                half = 2 * m + h
                if half >= Y_SLOTS:
                    pe.wait_ge(prod_ready, half - Y_SLOTS + 1)
                for t in range(2 * h, min(2 * h + 2, tiles_of(c, r))):
                    mm = nc.tensor.matmul(y_ps[half % Y_SLOTS][:, t - 2 * h, :],
                                          m_stack[:, k % STACK_SLOTS, m % PQ // CH, m % CH, TCOLS * t:TCOLS * t + TCOLS],
                                          x_stack[:, CH * r + t, :], start=True, stop=True)
                mm.then_inc(y_ready, 1)

            def sum_quad(m, tiles):
                k = m % QZ
                if k == 0 and m:
                    pe.wait_ge(z_copied, m // QZ)
                if m == QZ * (ZC - 1):
                    pe.wait_ge(dense_landed, 16 * CH)
                    for q in range(CH):
                        nc.tensor.matmul(z_ps[DIM * q:DIM * q + DIM, :], sel_dense_sb[:, q, :], dense_sb[:, :],
                                         start=True, stop=False)
                pe.wait_ge(prod_ready, 2 * m + 2)
                for t in range(tiles):
                    first = m < QZ * (ZC - 1) and (k == 0 or (m == 1 and t == CH - 1))
                    last = k == QZ - 1 or m == QUADS - 1 or (m == QUADS - 2 and t == CH - 1)
                    mm = nc.tensor.matmul(z_ps[DIM * t:DIM * t + DIM, :],
                                          sel_z_sb[:, CH * (QZ - 1 - k):CH * (QZ - 1 - k) + DIM],
                                          prod[:, m % PROD_SLOTS, t, :], start=first,
                                          stop=last)
                mm.then_inc(quad_summed, 1)

            def hidden1(zc, n):
                pe.wait_ge(z_copied, zc + 1)
                mm = nc.tensor.matmul(h1_ps[n], w1_sb[:, zc, P * n:P * n + P], z_sb[:, zc, :],
                                      start=(zc == AHEAD), stop=(zc == ZC - 1))
                if zc == ZC - 1:
                    mm.then_inc(h1_ready, 1)

            def hidden1_ahead(n):
                if n == 0:
                    pe.wait_ge(w1_landed, 16)
                    pe.wait_ge(z_copied, AHEAD)
                pe.wait_ge(emptied, ahead_done(n) - 1)
                for zc in range(AHEAD):
                    mm = nc.tensor.matmul(turn_ps[:, :], w1_sb[:, zc, P * n:P * n + P], z_sb[:, zc, :],
                                          start=(zc == 0), stop=(zc == AHEAD - 1))
                mm.then_inc(filled, 1)

            pe.wait_ge(ident_landed, 32)
            pe.wait_ge(consts_rounded, 2)
            for c in range(LC):
                for i in range(CH * c, CH * c + CH):
                    look_up(i)
                turn_looked(c)
            unsummed = []
            pe.wait_ge(sel_landed, 32)
            for what, *at in ORDER:
                if what == "turn":
                    turn_step(*at)
                elif what == "ahead":
                    hidden1_ahead(*at)
                if what != "quad":
                    continue
                m, c, r = at
                bilinear(m, c, r, 0)
                if len(unsummed) == 2:
                    sum_quad(*unsummed.pop(0))
                bilinear(m, c, r, 1)
                unsummed.append((m, tiles_of(c, r)))
            pe.wait_ge(emptied, LC + len(FILLS))
            hidden1(AHEAD, 2)
            sum_quad(*unsummed.pop(0))
            hidden1(AHEAD + 1, 2)
            pe.wait_ge(prod_ready, last_half - 1)
            hidden1(AHEAD, 0)
            sum_quad(*unsummed.pop(0))
            for n in (0, 1, 3):
                for zc in range(AHEAD, ZC - 1):
                    if (zc, n) != (AHEAD, 0):
                        hidden1(zc, n)
            for n in range(NB1):
                hidden1(ZC - 1, n)
            pe.wait_ge(tail_landed, 16 * 4)
            for k in range(NB1):
                pe.wait_ge(h1_relu, k + 1)
                for n in range(NB2):
                    mm = nc.tensor.matmul(h2_ps[n], w2_sb[:, k, P * n:P * n + P], h1_sb[:, k, :],
                                          start=(k == 0), stop=(k == NB1 - 1))
                    if k == NB1 - 1:
                        mm.then_inc(h2_ready, 1)
            for n in range(NB2):
                pe.wait_ge((relu2_act, relu2_dve)[n], 1)
                mm = nc.tensor.matmul(z_ps[0:1, :], w3_sb[:, n:n + 1], h2_sb[:, n, :], start=(n == 0), stop=(n == NB2 - 1))
            mm.then_inc(logit_ready, 1)


def layouts(w_top1, dense_ctx, bilinear):
    pair = {}
    for i in range(FIELDS):
        for j in range(i + 1, FIELDS):
            pair[i, j] = len(pair)
    m_raw = np.zeros((CH, DIM, PIECES * BLK, CH, CH, DIM), bilinear.dtype)
    w1 = np.zeros((ZC * P, w_top1.shape[1]), w_top1.dtype)
    for c in range(CHUNKS):
        for j in range(CH):
            for i in range(CH * c + j):
                m, t = first_quad(c) + i // CH, i % CH
                a, b = FIELD_ORDER[i], FIELD_ORDER[CH * c + j]
                p = pair[min(a, b), max(a, b)]
                m_raw[m % CH, :, m // CH, t, j] = bilinear[p] if a < b else bilinear[p].T
                w1[P * (m // QZ) + DIM * t + CH * (m % QZ) + j] = w_top1[p]
    for f in range(DENSE):
        w1[P * (ZC - 1) + DIM * (f // CH) + DIM - CH + f % CH] = w_top1[len(pair) + f]
    dense_t = np.ascontiguousarray(dense_ctx.T.reshape(CH, CH, BATCH).transpose(1, 0, 2))
    return m_raw.reshape(P, PIECES * BLK, QCOLS), w1, dense_t


def small_tables(tables):
    small = np.zeros((P * KT, len(tables), DIM), tables[0].dtype)
    for n, table in enumerate(tables):
        small[:SMALL, n] = table
    return small.reshape(P, KT, len(tables), DIM).transpose(0, 2, 1, 3)


def selectors():
    sel_z = np.zeros((P, 2 * DIM - CH), np.float32)
    sel_dense = np.zeros((P, CH, DIM), np.float32)
    for p in range(P):
        sel_z[p, DIM - CH + p // DIM] = 1
    for q in range(CH):
        for s in range(CH):
            sel_dense[DIM * s + q, q, DIM - CH + s] = 1
    sel_emb = np.zeros((P, 2 * P - DIM), np.float32)
    for p in range(H):
        sel_emb[p, P - DIM + p % DIM] = 1
    row_of = np.arange(P * KT, dtype=np.float32).reshape(P, KT)
    return np.eye(P, dtype=np.float32), sel_z, sel_dense, sel_emb, row_of


def kernel(**inputs):
    import concourse.bacc as _bacc
    from concourse.bass_utils import run_bass_kernel_spmd as _run

    given = {name: np.asarray(a) for name, a in inputs.items()}
    m_raw, w1, dense_t = layouts(given["W_top1"], given["dense_ctx"], given["L0_rec_bilinear_matrices"])
    ident, sel_z, sel_dense, sel_emb, row_of = selectors()
    laid = {"ids": given["ids"], "ids_rows": given["ids"].T[LOOKED].reshape(LC, CH * BATCH)}
    laid["small"] = small_tables([given[f"tbl_{f}"] for f in LOOKED])
    for f in FIELD_ORDER[len(LOOKED):]:
        laid[f"tbl_{f}"] = given[f"tbl_{f}"]
    laid["m_raw"] = m_raw
    laid["w1"] = w1
    laid["b1"] = given["b_top1"].reshape(NB1, P).T
    laid["w2"] = given["W_top2"]
    laid["b2"] = given["b_top2"].reshape(NB2, P).T
    laid["w3"] = given["W_top3"].reshape(NB2, P).T
    laid["dense_t"] = dense_t
    laid["ident"] = ident
    laid["sel_z"] = sel_z
    laid["sel_dense"] = sel_dense
    laid["sel_emb"] = sel_emb
    laid["row_of"] = row_of

    nc = _bacc.Bacc("TRN2", target_bir_lowering=False, num_devices=1)
    arrays, aps = {}, {}
    for name, a in laid.items():
        a = np.ascontiguousarray(a)
        arrays[f"in_{name}"] = a
        aps[name] = nc.dram_tensor(f"in_{name}", a.shape, mybir.dt.from_np(a.dtype), kind="ExternalInput").ap()
    out = nc.dram_tensor("out_0", (BATCH, 1), F32, kind="ExternalOutput").ap()
    build(nc, aps["ids"], aps["ids_rows"], aps["small"], aps["row_of"],
          {f: aps[f"tbl_{f}"] for f in FIELD_ORDER[len(LOOKED):]}, aps["m_raw"], aps["w1"], aps["b1"], aps["w2"],
          aps["b2"], aps["w3"], aps["dense_t"], aps["ident"], aps["sel_z"], aps["sel_dense"], aps["sel_emb"], out)
    r = _run(nc, [arrays], core_ids=[0])
    return r.results[0]["out_0"]
```

```python
from contextlib import ExitStack

import numpy as np

import concourse.bass as bass
from concourse import mybir

F32 = mybir.dt.float32
F32R = mybir.dt.float32r
I32 = mybir.dt.int32
ALU = mybir.AluOpType
ACT = mybir.ActivationFunctionType

P = 128
H = P // 2
BATCH, FIELDS, DIM = 512, 40, 32
DENSE = 16
HID1, HID2 = 512, 256
BT = BATCH // P
CH = P // DIM
CHUNKS = FIELDS // CH
QUADS = CHUNKS * (CHUNKS + 1) // 2
QZ = DIM // CH
ZC = -(-(QUADS + 1) // QZ)
NB1, NB2 = HID1 // P, HID2 // P
BLK = 2
PQ = CH * BLK
PIECES = -(-QUADS // PQ)
TCOLS = CH * DIM
QCOLS = CH * TCOLS
SMALL = 1000
LOOKED = [18, 19, 20, 21, 25, 26, 28, 29]
LOOKED_CHUNKS = [0, 2]
GATHERED_CHUNKS = [c for c in range(CHUNKS) if c not in LOOKED_CHUNKS]
LOOKED_AT = [CH * c + j for c in LOOKED_CHUNKS for j in range(CH)]
GATHERED_FIELDS = [f for f in range(FIELDS) if f not in LOOKED]
FIELD_ORDER = [LOOKED[LOOKED_AT.index(i)] if i in LOOKED_AT
               else GATHERED_FIELDS[i - sum(at < i for at in LOOKED_AT)] for i in range(FIELDS)]
KT = -(-SMALL // P)
KT_DVE = 7
KT_ACT = KT - KT_DVE
ONEHOT_SLOTS = 8
ONEHOT_ACT_SLOTS = 4

GATHER_SLOTS, EMB_SLOTS = 3, 2
PROD_SLOTS = 3
STACK_SLOTS = 2
RAW_SLOTS = 1
PART_SLOTS = 1
STEPS = 1 + CH // 2
Y_SLOTS = 3
EARLY_HALVES = 6
ROUNDS = [[0, 1], [2, 3], [4]]
LAST = [zcs[-1] for zcs in ROUNDS]
AHEAD = LAST[-1] + 1
STAGE_OF = 7
POOL_ROWS, POOL_PIECES = (9,), (6,)
LATE_GATHERS = (8, 9)
assert (QUADS + 1) % QZ == 0


def first_quad(c):
    return c * (c + 1) // 2


def steps_done(c, s):
    return FILLS.index(("emb", c) if c in LOOKED_CHUNKS else ("turn", c, s)) + 1


def z_place(m):
    return divmod(m + 1, QZ)


def last_in_chunk(m, t):
    later = [n for n in range(m + 1, QUADS) if z_place(n)[0] == z_place(m)[0]]
    return not any(t < tiles_of(*quad_at(n)) for n in later)


def quad_at(m):
    c = max(c for c in range(CHUNKS) if first_quad(c) <= m)
    return c, m - first_quad(c)


def prod_slot(m):
    return (0, 2, 0)[m] if m < 3 else (m - 2) % PROD_SLOTS


def y_slot(half):
    return half % Y_SLOTS if half >= EARLY_HALVES else half % (Y_SLOTS - 1)


def y_free(half):
    return 1 + max([h for h in range(max(0, half - Y_SLOTS), half) if y_slot(h) == y_slot(half)], default=-1)


def ahead_done(n, r):
    return FILLS.index(("ahead", n, LAST[r])) + 1


def tiles_of(c, r):
    return min(CH, CH * c + CH - 1 - CH * r)


PLAN = """
    small 0, small 1, cols 0, small 2, cols 1, piece_hi 0, small 3, consts, cols 2, look 0, look 1, piece_lo 0
    look 2, small 4, small 5, cols 3, cols 4, look 3, cols 5, emb 0, small 6, look 4, piece_hi 1, turn 1 0
    cols 6, split_hi 1, small 7, look 5, look 6, split_lo 1, quad 0, turn 1 1, cols 7, turn 1 2, look 7, quad 1
    emb 2, piece_lo 1, quad 2
    turn 3 0, quad 3, split_hi 3, split_lo 3, quad 4, quad 5
    quad 6, turn 3 1, quad 7, turn 3 2, quad 8
    piece_hi 2, z 0, rows 8 0, split_hi 4, piece_lo 2, split_lo 4, turn 4 0, quad 9, turn 4 1, quad 10, quad 11
    turn 4 2, quad 12, quad 13, quad 14
    turn 5 0, quad 15, split_hi 5, rows 8 1, quad 16, z 1, rows 8 2, split_lo 5, piece_hi 3, piece_lo 3
    ahead 0 0, ahead 0 1, quad 17
    turn 5 1, quad 18, turn 5 2, quad 19, ahead 1 0, rows 8 3, ahead 1 1, split_hi 6, quad 20
    turn 6 0, split_lo 6, quad 21, quad 22, rows 9 0, turn 6 1, piece_hi 4, quad 23
    z 2, quad 24, piece_lo 4, ahead 2 0, ahead 2 1, quad 25, turn 6 2, split_hi 7, quad 26
    quad 27, split_lo 7, turn 7 0, quad 28, turn 7 1, quad 29
    quad 30, quad 31, ahead 3 0, ahead 3 1, piece_hi 5, quad 32
    z 3, turn 7 2, quad 33, piece_lo 5, split_hi 8, quad 34, ahead 0 2, ahead 0 3, quad 35
    turn 8 0, quad 36, rows 9 1, ahead 1 2, ahead 1 3, split_lo 8, rows 9 2, quad 37, turn 8 1, quad 38
    quad 39, ahead 2 2, rows 9 3, ahead 2 3, quad 40, piece_hi 6, quad 41
    piece_lo 6, z 4, ahead 3 2, ahead 3 3, quad 42, turn 8 2, split_hi 9, quad 43, turn 9 0, quad 44
    ahead 0 4, quad 45, quad 46, split_lo 9, turn 9 1, quad 47
    quad 48, z 5, ahead 1 4, quad 49, turn 9 2, quad 50
    ahead 2 4, quad 51, quad 52, ahead 3 4, quad 53
    quad 54
"""


def plan(text):
    for item in text.replace("\n", ",").split(","):
        if item.strip():
            what, *at = item.split()
            at = [int(a) for a in at]
            yield (what, *at, *quad_at(*at)) if what == "quad" else (what, *at)


ORDER = list(plan(PLAN))
FILLS = [what for what in ORDER if what[0] in ("emb", "turn") or (what[0] == "ahead" and what[2] in LAST)]


def build(nc, ids, ids_rows, small, row_of, tables, m_raw, w1, b1, w2, b2, w3, dense_t, ident, sel_z, sel_dense, sel_emb, out):
    with ExitStack() as ctx:
        def sb(name, shape, dt=F32):
            return ctx.enter_context(nc.sbuf_tensor(name, shape, dt))

        def sem(name):
            return ctx.enter_context(nc.semaphore(name))

        ids_sb = sb("ids_sb", [P, BT * FIELDS], I32)
        gathered = sb("gathered", [P, GATHER_SLOTS, BT, CH * DIM])
        split = sb("split", [P, BT, CH, 2, DIM], F32R)
        emb_t = sb("emb_t", [P, EMB_SLOTS, BATCH])
        x_stack = sb("x_stack", [P, FIELDS - 1, BATCH], F32R)
        raw = sb("raw", [P, RAW_SLOTS, BLK, QCOLS])
        m_hi = sb("m_hi", [P, PART_SLOTS, BLK, QCOLS], F32R)
        m_lo = sb("m_lo", [P, PART_SLOTS, BLK, QCOLS], F32R)
        m_stack = sb("m_stack", [P, STACK_SLOTS, BLK, CH, QCOLS], F32R)
        prod = sb("prod", [P, PROD_SLOTS, CH, BATCH])
        z_sb = sb("z_sb", [P, ZC, BATCH])
        h1_ahead = sb("h1_ahead", [P, NB1, BATCH])
        w1_sb = sb("w1_sb", [P, ZC, HID1])
        w2_sb = sb("w2_sb", [P, NB1, HID2])
        w3_sb = sb("w3_sb", [P, NB2])
        b1_sb = sb("b1_sb", [P, NB1])
        b2_sb = sb("b2_sb", [P, NB2])
        dense_sb = sb("dense_sb", [P, BATCH])
        ident_sb = sb("ident_sb", [P, P])
        ident_r = sb("ident_r", [P, P], F32R)
        sel_z_sb = sb("sel_z_sb", [P, 2 * DIM - CH])
        sel_dense_sb = sb("sel_dense_sb", [P, CH, DIM])
        row_of_sb = sb("row_of_sb", [P, 2 * KT])
        sel_emb_sb = sb("sel_emb_sb", [P, 2 * P - DIM])
        sel_emb_r = sb("sel_emb_r", [P, 2 * P - DIM], F32R)
        y_sb = emb_t[0:1, CHUNKS % EMB_SLOTS, :]
        looked_ids = prod[:, :, :, :].rearrange("p a b c -> p (a b c)")[:, 0:len(LOOKED) * BATCH].bitcast(I32)
        small_sb = z_sb[:, :, :].rearrange("p a b -> p (a b)")[:, 0:len(LOOKED) * KT * DIM].rearrange(
            "p (f k d) -> p f k d", f=len(LOOKED), k=KT)
        parts_at, onehot_at = 4 * CH, 6 * CH
        small_parts = x_stack[:, parts_at:onehot_at, :].rearrange("p a b -> p (a b)").rearrange(
            "p (f k h d) -> p f k h d", f=len(LOOKED), k=KT, h=2)
        onehot = x_stack[:, onehot_at:onehot_at + ONEHOT_SLOTS, :]
        onehot_act = x_stack[:, onehot_at + ONEHOT_SLOTS:onehot_at + ONEHOT_SLOTS + ONEHOT_ACT_SLOTS, :]
        h1_sb = prod[:, prod_slot(QUADS - 3), :, :]
        h2_sb = prod[:, prod_slot(QUADS - 2), 0:NB2, :]

        y_ps = [ctx.enter_context(nc.psum_tensor(f"y_ps{s}", [P, 2, BATCH], F32)) for s in range(Y_SLOTS)]
        z_ps = ctx.enter_context(nc.psum_tensor("z_ps", [P, BATCH], F32))
        turn_ps = ctx.enter_context(nc.psum_tensor("turn_ps", [P, BATCH], F32))
        look_ps = [y_ps[Y_SLOTS - 1][:, b, :] for b in range(2)]
        last_half = 2 * QUADS - 1
        late = y_ps[y_slot(last_half - 2)]
        h1_ps = [late[:, 0, :], late[:, 1, :], turn_ps[:, :], y_ps[y_slot(last_half)][:, 1, :]]
        h2_ps = [y_ps[y_slot(last_half - 1)][:, b, :] for b in range(NB2)]

        ids_landed = sem("ids_landed")
        ident_landed = sem("ident_landed")
        sel_landed = sem("sel_landed")
        w1_landed = sem("w1_landed")
        tail_landed = sem("tail_landed")
        dense_zeroed = sem("dense_zeroed")
        dense_landed = sem("dense_landed")
        rows_landed = [sem(f"rows_landed{c}") for c in range(CHUNKS)]
        raw_landed = [sem(f"raw_landed{s}") for s in range(RAW_SLOTS)]
        stack_landed = [sem(f"stack_landed{s}") for s in range(STACK_SLOTS)]
        ids_rows_landed = [sem(f"ids_rows_landed{n}") for n in range(len(LOOKED) // 2)]
        small_landed = [sem(f"small_landed{c}") for c in LOOKED_CHUNKS]
        row_of_landed = sem("row_of_landed")
        consts_rounded = sem("consts_rounded")
        small_hi, small_lo = sem("small_hi"), sem("small_lo")
        onehot_ready = sem("onehot_ready")
        onehot_distance = sem("onehot_distance")
        onehot_act_ready = sem("onehot_act_ready")
        onehot_used = sem("onehot_used")
        looked_copied = sem("looked_copied")
        rows_hi = sem("rows_hi")
        rows_lo = sem("rows_lo")
        m_hi_done = sem("m_hi_done")
        m_lo_done = sem("m_lo_done")
        filled = sem("filled")
        emptied = sem("emptied")
        y_ready = sem("y_ready")
        prod_ready = sem("prod_ready")
        quad_summed = sem("quad_summed")
        z_copied = sem("z_copied")
        h1_ready = sem("h1_ready")
        merged = sem("merged")
        h1_added = sem("h1_added")
        h1_relu = sem("h1_relu")
        h2_ready = sem("h2_ready")
        relu2_act, relu2_dve = sem("relu2_act"), sem("relu2_dve")
        logit_ready = sem("logit_ready")
        logit_copied = sem("logit_copied")
        out_written = sem("out_written")

        ROWS_INC = 16 * CH * BT
        STACK_INC = 16 * CH * 4

        block = ctx.enter_context(nc.Block())

        @block.sync
        def _(sp):
            def load_raw(k):
                sp.dma_start(raw[:, k % RAW_SLOTS, :, :], m_raw[:, BLK * k:BLK * k + BLK, :]).then_inc(raw_landed[k % RAW_SLOTS], 16)

            sp.dma_start(ids_sb[:, :], ids.rearrange("(t p) f -> p t f", p=P)).then_inc(ids_landed, 16)
            sp.dma_start(row_of_sb[:, :], row_of).then_inc(row_of_landed, 16)
            for c in range(len(LOOKED_CHUNKS)):
                sp.dma_start(small_sb[:, CH * c:CH * c + CH, :, :], small[c]).then_inc(small_landed[c], 16)
                for i in range(CH * c, CH * c + CH, 2):
                    sp.dma_start(looked_ids[:, BATCH * i:BATCH * (i + 2)],
                                 ids_rows[i // 2:i // 2 + 1, :].broadcast_to([P, 2 * BATCH])
                                 ).then_inc(ids_rows_landed[i // 2], 16)
                if c == 0:
                    load_raw(0)
                    sp.dma_start(ident_sb[:, :], ident).then_inc(ident_landed, 16)
                    sp.dma_start(sel_emb_sb[:, :], sel_emb).then_inc(ident_landed, 16)
            sp.dma_start(sel_z_sb[:, :], sel_z).then_inc(sel_landed, 16)
            sp.dma_start(sel_dense_sb[:, :, :], sel_dense).then_inc(sel_landed, 16)
            for k in range(PIECES):
                sp.wait_ge(m_lo_done, k + 1)
                if k + RAW_SLOTS < PIECES:
                    load_raw(k + RAW_SLOTS)
                if k >= STACK_SLOTS:
                    sp.wait_ge(y_ready, 2 * PQ * (k - STACK_SLOTS + 1))
                for s in range(CH):
                    src = slice(DIM * s, DIM * s + DIM)
                    for copy in range(4):
                        part = (m_hi, m_hi, m_lo, m_lo)[copy]
                        sp.dma_start(m_stack[DIM * copy:DIM * copy + DIM, k % STACK_SLOTS, :, s, :].bitcast(F32),
                                     part[src, k % PART_SLOTS, :, :].bitcast(F32)
                                     ).then_inc(stack_landed[k % STACK_SLOTS], 16)
                if k == 0:
                    sp.dma_start(w1_sb[:, :, :], w1.rearrange("(c p) n -> p c n", p=P)).then_inc(w1_landed, 16)
                    sp.wait_ge(dense_zeroed, 1)
                    for s in range(CH):
                        sp.dma_start(dense_sb[DIM * s:DIM * s + CH, :], dense_t[s]).then_inc(dense_landed, 16)
                    sp.dma_start(w2_sb[:, :, :], w2.rearrange("(c p) n -> p c n", p=P)).then_inc(tail_landed, 16)
                    sp.dma_start(w3_sb[:, :], w3).then_inc(tail_landed, 16)
                    sp.dma_start(b1_sb[:, :], b1).then_inc(tail_landed, 16)
                    sp.dma_start(b2_sb[:, :], b2).then_inc(tail_landed, 16)
            sp.wait_ge(logit_copied, 1)
            sp.dma_start(out.rearrange("(a b) o -> a (b o)", a=1), y_sb).then_inc(out_written, 16)
            sp.wait_ge(out_written, 16)

        stage = gathered[:, GATHERED_CHUNKS.index(STAGE_OF) % GATHER_SLOTS, :, :].rearrange("p t d -> p (t d)")

        def lo_of_piece(engine, unit, k):
            engine.wait_ge(m_hi_done, k + 1)
            unit.tensor_tensor(m_lo[:, k % PART_SLOTS, :, :], raw[:, k % RAW_SLOTS, :, :],
                               m_hi[:, k % PART_SLOTS, :, :].bitcast(F32), ALU.subtract).then_inc(m_lo_done, 1)

        def lo_of_rows(engine, unit, c):
            engine.wait_ge(rows_hi, GATHERED_CHUNKS.index(c) + 1)
            unit.tensor_tensor(split[:, :, :, 1, :],
                               gathered[:, GATHERED_CHUNKS.index(c) % GATHER_SLOTS, :, :].rearrange("p t (j d) -> p t j d", d=DIM),
                               split[:, :, :, 0, :].bitcast(F32), ALU.subtract).then_inc(rows_lo, 1)

        @block.gpsimd
        def _(pool):
            pool.memset(dense_sb[:, :], 0.0).then_inc(dense_zeroed, 1)
            pool.wait_ge(ids_landed, 16)

            def gather(c, j):
                g = GATHERED_CHUNKS.index(c)
                if j == 0 and g >= GATHER_SLOTS:
                    pool.wait_ge(filled, steps_done(GATHERED_CHUNKS[g - GATHER_SLOTS], 0))
                    pool.wait_ge(rows_lo, g - GATHER_SLOTS + 1)
                f = FIELD_ORDER[CH * c + j]
                for t in range(BT):
                    pool.indirect_dma_start(
                        out=gathered[:, g % GATHER_SLOTS, t, DIM * j:DIM * j + DIM], out_offset=None,
                        in_=tables[f][:, :],
                        in_offset=bass.IndirectOffsetOnAxis(
                            ap=ids_sb[:, FIELDS * t + f:FIELDS * t + f + 1], axis=0),
                    ).then_inc(rows_landed[c], 16)

            for c in GATHERED_CHUNKS:
                for j in range(0 if c in LATE_GATHERS else CH):
                    gather(c, j)
            for what, *at in ORDER:
                if what == "rows":
                    gather(*at)
                elif what == "split_lo" and at[0] in POOL_ROWS:
                    lo_of_rows(pool, nc.gpsimd, *at)
                elif what == "piece_lo" and at[0] in POOL_PIECES:
                    lo_of_piece(pool, nc.gpsimd, *at)
                elif what == "ahead" and at[1] in LAST[1:]:
                    n, zc = at
                    pool.wait_ge(emptied, ahead_done(n, LAST.index(zc)))
                    nc.gpsimd.tensor_tensor(h1_ahead[:, n, :], stage, h1_ahead[:, n, :], ALU.add).then_inc(merged, 1)

        @block.scalar
        def _(act):
            def m_part(k):
                act.wait_ge(raw_landed[k % RAW_SLOTS], 16 * (k // RAW_SLOTS + 1))
                if k >= PART_SLOTS:
                    j = k - PART_SLOTS
                    act.wait_ge(stack_landed[j % STACK_SLOTS], STACK_INC * (j // STACK_SLOTS + 1))
                nc.scalar.copy(m_hi[:, k % PART_SLOTS, :, :], raw[:, k % RAW_SLOTS, :, :]).then_inc(m_hi_done, 1)

            def split_rows(c):
                act.wait_ge(rows_landed[c], ROWS_INC)
                g = GATHERED_CHUNKS.index(c)
                if g:
                    act.wait_ge(filled, steps_done(GATHERED_CHUNKS[g - 1], STEPS - 1))
                nc.scalar.copy(split[:, :, :, 0, :],
                               gathered[:, GATHERED_CHUNKS.index(c) % GATHER_SLOTS, :, :].rearrange("p t (j d) -> p t j d", d=DIM)
                               ).then_inc(rows_hi, 1)

            def copy_emb(c):
                act.wait_ge(filled, steps_done(c, 0))
                if c >= EMB_SLOTS:
                    act.wait_ge(prod_ready, 2 * first_quad(c - EMB_SLOTS + 1))
                nc.scalar.copy(emb_t[:, c % EMB_SLOTS, :], turn_ps[:, :]).then_inc(emptied, 1)

            def copy_stack(i, parts):
                for copy in range(2):
                    last = nc.scalar.copy(x_stack[H * copy:H * copy + H, i, :], parts)
                return last

            def onehots(f):
                if f == 0:
                    act.wait_ge(row_of_landed, 16)
                if f % 2 == 0:
                    act.wait_ge(ids_rows_landed[f // 2], 16)
                for k in range(KT_DVE, KT):
                    a = KT_ACT * f + k - KT_DVE
                    if a >= ONEHOT_ACT_SLOTS:
                        f0, k0 = divmod(a - ONEHOT_ACT_SLOTS, KT_ACT)
                        act.wait_ge(onehot_used, KT * f0 + KT_DVE + k0 + 1)
                    nc.scalar.activation(onehot_act[:, a % ONEHOT_ACT_SLOTS, :], looked_ids[:, BATCH * f:BATCH * (f + 1)],
                                         ACT.Abs, bias=row_of_sb[:, KT + k:KT + k + 1]).then_inc(onehot_distance, 1)
                for k in range(KT_DVE, KT):
                    a = KT_ACT * f + k - KT_DVE
                    act.wait_ge(onehot_distance, a + 1)
                    nc.scalar.activation(onehot_act[:, a % ONEHOT_ACT_SLOTS, :],
                                         onehot_act[:, a % ONEHOT_ACT_SLOTS, :].bitcast(F32), ACT.Relu,
                                         scale=-1.0, bias=1.0).then_inc(onehot_act_ready, 1)

            for what, *at in ORDER:
                if what == "small":
                    f = at[0]
                    act.wait_ge(small_landed[f // CH], 16)
                    nc.scalar.copy(small_parts[:, f, :, 0, :], small_sb[:, f, :, :]).then_inc(small_hi, 1)
                elif what == "consts":
                    act.wait_ge(ident_landed, 32)
                    nc.scalar.copy(ident_r[:, :], ident_sb[:, :]).then_inc(consts_rounded, 1)
                    nc.scalar.copy(sel_emb_r[:, :], sel_emb_sb[:, :]).then_inc(consts_rounded, 1)
                elif what == "cols":
                    onehots(*at)
                elif what == "look":
                    i = at[0]
                    act.wait_ge(onehot_used, KT * (i + 1))
                    copy_stack(LOOKED_AT[i], look_ps[i % len(look_ps)][0:H, :]).then_inc(looked_copied, 1)
                elif what == "emb":
                    copy_emb(*at)
                elif what == "split_hi":
                    split_rows(*at)
                elif what == "turn":
                    c, s = at
                    if s == 0:
                        copy_emb(c)
                        continue
                    act.wait_ge(filled, steps_done(c, s))
                    for j in range(2 * s - 2, min(2 * s, FIELDS - 1 - CH * c)):
                        last = copy_stack(CH * c + j, turn_ps[H * (j % 2):H * (j % 2) + H, :])
                    last.then_inc(emptied, 1)
                elif what == "ahead":
                    n, zc = at
                    if zc not in LAST:
                        continue
                    r = LAST.index(zc)
                    act.wait_ge(filled, ahead_done(n, r))
                    if r:
                        if (n, r) == (0, 1):
                            act.wait_ge(rows_lo, GATHERED_CHUNKS.index(STAGE_OF) + 1)
                        else:
                            act.wait_ge(merged, NB1 * (r - 1) + n)
                        nc.scalar.copy(stage, turn_ps[:, :]).then_inc(emptied, 1)
                        continue
                    if n == 0:
                        act.wait_ge(tail_landed, 16 * 4)
                    nc.scalar.activation(h1_ahead[:, n, :], turn_ps[:, :], ACT.Identity,
                                         bias=b1_sb[:, n:n + 1]).then_inc(emptied, 1)
                elif what == "piece_hi":
                    m_part(*at)
                elif what == "z":
                    act.wait_ge(quad_summed, QZ * (at[0] + 1) - 1)
                    nc.scalar.copy(z_sb[:, at[0], :], z_ps[:, :]).then_inc(z_copied, 1)
            act.wait_ge(quad_summed, QUADS)
            nc.scalar.copy(z_sb[:, ZC - 1, :], z_ps[:, :]).then_inc(z_copied, 1)
            for n in range(NB1):
                act.wait_ge(h1_added, n + 1)
                nc.scalar.activation(h1_sb[:, n, :], h1_sb[:, n, :], ACT.Relu).then_inc(h1_relu, 1)
            act.wait_ge(h2_ready, 1)
            nc.scalar.activation(h2_sb[:, 0, :], h2_ps[0], ACT.Relu, bias=b2_sb[:, 0:1]).then_inc(relu2_act, 1)
            act.wait_ge(logit_ready, 1)
            nc.scalar.copy(y_sb, z_ps[0:1, :]).then_inc(logit_copied, 1)

        @block.vector
        def _(dve):
            def look_up(f):
                dve.wait_ge(small_hi, f + 1)
                nc.vector.tensor_tensor(small_parts[:, f, :, 1, :], small_sb[:, f, :, :],
                                        small_parts[:, f, :, 0, :].bitcast(F32), ALU.subtract).then_inc(small_lo, 1)
                if f % 2 == 0:
                    dve.wait_ge(ids_rows_landed[f // 2], 16)
                for k in range(KT_DVE):
                    d = KT_DVE * f + k
                    if d >= ONEHOT_SLOTS:
                        f0, k0 = divmod(d - ONEHOT_SLOTS, KT_DVE)
                        dve.wait_ge(onehot_used, KT * f0 + k0 + 1)
                    nc.vector.tensor_scalar(onehot[:, d % ONEHOT_SLOTS, :], looked_ids[:, BATCH * f:BATCH * (f + 1)],
                                            row_of_sb[:, k:k + 1], None, ALU.is_equal).then_inc(onehot_ready, 1)

            dve.wait_ge(row_of_landed, 16)
            for what, *at in ORDER:
                if what == "look":
                    look_up(*at)
                elif what == "split_lo" and at[0] not in POOL_ROWS:
                    lo_of_rows(dve, nc.vector, *at)
                elif what == "piece_lo" and at[0] not in POOL_PIECES:
                    lo_of_piece(dve, nc.vector, *at)
                if what != "quad":
                    continue
                m, c, r = at
                if r == 0:
                    dve.wait_ge(emptied, steps_done(c, 0))
                for h in range(2):
                    n = min(2, tiles_of(c, r) - 2 * h)
                    if h == 0 and m >= 2:
                        dve.wait_ge(quad_summed, max(1, m - PROD_SLOTS + 1))
                    dve.wait_ge(y_ready, 2 * m + h + 1)
                    nc.vector.tensor_tensor(prod[:, prod_slot(m), 2 * h:2 * h + n, :],
                                            y_ps[y_slot(2 * m + h)][:, 0:n, :],
                                            emb_t[:, c % EMB_SLOTS:c % EMB_SLOTS + 1, :].broadcast_to([P, n, BATCH]),
                                            ALU.mult).then_inc(prod_ready, 1)
            dve.wait_ge(merged, NB1 * (len(ROUNDS) - 1))
            for n in range(NB1):
                dve.wait_ge(h1_ready, n + 1)
                nc.vector.tensor_tensor(h1_sb[:, n, :], h1_ps[n], h1_ahead[:, n, :], ALU.add).then_inc(h1_added, 1)
            dve.wait_ge(h2_ready, 2)
            nc.vector.tensor_scalar(h2_sb[:, 1, :], h2_ps[1], b2_sb[:, 1:2], 0.0, ALU.add,
                                    ALU.max).then_inc(relu2_dve, 1)

        @block.tensor
        def _(pe):
            def turn_step(c, s):
                n = steps_done(c, s) - 1
                if n:
                    pe.wait_ge(emptied, n)
                if s == 0:
                    pe.wait_ge(rows_landed[c], ROWS_INC)
                if s == 1:
                    pe.wait_ge(rows_lo, GATHERED_CHUNKS.index(c) + 1)
                for t in range(BT):
                    cols = turn_ps[:, P * t:P * t + P]
                    if s == 0:
                        mm = nc.tensor.matmul(cols, gathered[:, GATHERED_CHUNKS.index(c) % GATHER_SLOTS, t, :], ident_sb[:, :],
                                              start=True, stop=True)
                    else:
                        rows = split[:, t, 2 * s - 2:2 * s, :, :].rearrange("p j h d -> p (j h d)")
                        mm = nc.tensor.matmul(cols, rows, ident_r[:, :], start=True, stop=True)
                mm.then_inc(filled, 1)

            def look_up(i):
                if i >= len(look_ps):
                    pe.wait_ge(looked_copied, i - len(look_ps) + 1)
                pe.wait_ge(small_lo, i + 1)
                for k in range(KT):
                    if k < KT_DVE:
                        n = KT_DVE * i + k
                        columns = onehot[:, n % ONEHOT_SLOTS, :]
                        pe.wait_ge(onehot_ready, n + 1)
                    else:
                        n = KT_ACT * i + k - KT_DVE
                        columns = onehot_act[:, n % ONEHOT_ACT_SLOTS, :]
                        pe.wait_ge(onehot_act_ready, n + 1)
                    mm = nc.tensor.matmul(look_ps[i % len(look_ps)][0:H, :],
                                          small_parts[:, i, k, :, :].rearrange("p h d -> p (h d)"),
                                          columns, start=(k == 0), stop=(k == KT - 1))
                    mm.then_inc(onehot_used, 1)

            def turn_looked(c):
                pe.wait_ge(looked_copied, CH * (LOOKED_CHUNKS.index(c) + 1))
                if steps_done(c, 0) > 1:
                    pe.wait_ge(emptied, steps_done(c, 0) - 1)
                for j in range(CH):
                    mm = nc.tensor.matmul(turn_ps[:, :], sel_emb_r[:, DIM * (CH - 1 - j):DIM * (CH - 1 - j) + P],
                                          x_stack[:, CH * c + j, :], start=(j == 0), stop=(j == CH - 1))
                mm.then_inc(filled, 1)

            def bilinear(m, c, r, h):
                k = m // PQ
                if h == 0 and m % PQ == 0:
                    pe.wait_ge(stack_landed[k % STACK_SLOTS], STACK_INC * (k // STACK_SLOTS + 1))
                if h == 0 and r == c:
                    pe.wait_ge(emptied, steps_done(c, STEPS - 1))
                half = 2 * m + h
                if y_free(half):
                    pe.wait_ge(prod_ready, y_free(half))
                for t in range(2 * h, min(2 * h + 2, tiles_of(c, r))):
                    mm = nc.tensor.matmul(y_ps[y_slot(half)][:, t - 2 * h, :],
                                          m_stack[:, k % STACK_SLOTS, m % PQ // CH, m % CH, TCOLS * t:TCOLS * t + TCOLS],
                                          x_stack[:, CH * r + t, :], start=True, stop=True)
                mm.then_inc(y_ready, 1)

            def sum_quad(m, tiles):
                zc, k = z_place(m)
                if m == 0:
                    pe.wait_ge(sel_landed, 32)
                    pe.wait_ge(dense_landed, 16 * CH)
                    for q in range(CH):
                        nc.tensor.matmul(z_ps[DIM * q:DIM * q + DIM, :], sel_dense_sb[:, q, :], dense_sb[:, :],
                                         start=True, stop=False)
                if k == 0:
                    pe.wait_ge(z_copied, zc)
                pe.wait_ge(prod_ready, 2 * m + 2)
                for t in range(tiles):
                    mm = nc.tensor.matmul(z_ps[DIM * t:DIM * t + DIM, :],
                                          sel_z_sb[:, CH * (QZ - 1 - k):CH * (QZ - 1 - k) + DIM],
                                          prod[:, prod_slot(m), t, :], start=(k == 0), stop=last_in_chunk(m, t))
                mm.then_inc(quad_summed, 1)

            def hidden1(zc, n):
                pe.wait_ge(z_copied, zc + 1)
                mm = nc.tensor.matmul(h1_ps[n], w1_sb[:, zc, P * n:P * n + P], z_sb[:, zc, :],
                                      start=(zc == AHEAD), stop=(zc == ZC - 1))
                if zc == ZC - 1:
                    mm.then_inc(h1_ready, 1)

            def hidden1_ahead(n, zc):
                r = [zc in zcs for zcs in ROUNDS].index(True)
                if n == 0 or zc == 0:
                    pe.wait_ge(w1_landed, 16)
                    pe.wait_ge(z_copied, zc + 1)
                if zc == ROUNDS[r][0]:
                    pe.wait_ge(emptied, ahead_done(n, r) - 1)
                mm = nc.tensor.matmul(turn_ps[:, :], w1_sb[:, zc, P * n:P * n + P], z_sb[:, zc, :],
                                      start=(zc == ROUNDS[r][0]), stop=(zc == LAST[r]))
                if zc == LAST[r]:
                    mm.then_inc(filled, 1)

            unsummed = []
            for what, *at in ORDER:
                if (what, *at) == FILLS[0]:
                    pe.wait_ge(ident_landed, 32)
                    pe.wait_ge(consts_rounded, 2)
                if what == "look":
                    look_up(*at)
                elif what == "emb":
                    turn_looked(*at)
                elif what == "turn":
                    turn_step(*at)
                elif what == "ahead":
                    hidden1_ahead(*at)
                if what != "quad":
                    continue
                m, c, r = at
                bilinear(m, c, r, 0)
                if len(unsummed) == 2:
                    sum_quad(*unsummed.pop(0))
                bilinear(m, c, r, 1)
                unsummed.append((m, tiles_of(c, r)))
            pe.wait_ge(emptied, len(FILLS))
            for zc in range(AHEAD, ZC - 2):
                hidden1(zc, 2)
            sum_quad(*unsummed.pop(0))
            hidden1(ZC - 2, 2)
            pe.wait_ge(prod_ready, last_half - 1)
            hidden1(AHEAD, 0)
            sum_quad(*unsummed.pop(0))
            for n in (0, 1, 3):
                for zc in range(AHEAD, ZC - 1):
                    if (zc, n) != (AHEAD, 0):
                        hidden1(zc, n)
            for n in range(NB1):
                hidden1(ZC - 1, n)
            pe.wait_ge(tail_landed, 16 * 4)
            for k in range(NB1):
                pe.wait_ge(h1_relu, k + 1)
                for n in range(NB2):
                    mm = nc.tensor.matmul(h2_ps[n], w2_sb[:, k, P * n:P * n + P], h1_sb[:, k, :],
                                          start=(k == 0), stop=(k == NB1 - 1))
                    if k == NB1 - 1:
                        mm.then_inc(h2_ready, 1)
            for n in range(NB2):
                pe.wait_ge((relu2_act, relu2_dve)[n], 1)
                mm = nc.tensor.matmul(z_ps[0:1, :], w3_sb[:, n:n + 1], h2_sb[:, n, :], start=(n == 0), stop=(n == NB2 - 1))
            mm.then_inc(logit_ready, 1)


def layouts(w_top1, dense_ctx, bilinear):
    pair = {}
    for i in range(FIELDS):
        for j in range(i + 1, FIELDS):
            pair[i, j] = len(pair)
    m_raw = np.zeros((CH, DIM, PIECES * BLK, CH, CH, DIM), bilinear.dtype)
    w1 = np.zeros((ZC * P, w_top1.shape[1]), w_top1.dtype)
    for c in range(CHUNKS):
        for j in range(CH):
            for i in range(CH * c + j):
                m, t = first_quad(c) + i // CH, i % CH
                a, b = FIELD_ORDER[i], FIELD_ORDER[CH * c + j]
                p = pair[min(a, b), max(a, b)]
                m_raw[m % CH, :, m // CH, t, j] = bilinear[p] if a < b else bilinear[p].T
                zc, k = z_place(m)
                w1[P * zc + DIM * t + CH * k + j] = w_top1[p]
    for f in range(DENSE):
        w1[DIM * (f // CH) + f % CH] = w_top1[len(pair) + f]
    dense_t = np.ascontiguousarray(dense_ctx.T.reshape(CH, CH, BATCH).transpose(1, 0, 2))
    return m_raw.reshape(P, PIECES * BLK, QCOLS), w1, dense_t


def small_tables(tables):
    small = np.zeros((P * KT, len(tables), DIM), tables[0].dtype)
    for n, table in enumerate(tables):
        small[:SMALL, n] = table
    return small.reshape(P, KT, len(LOOKED_CHUNKS), CH, DIM).transpose(2, 0, 3, 1, 4)


def selectors():
    sel_z = np.zeros((P, 2 * DIM - CH), np.float32)
    sel_dense = np.zeros((P, CH, DIM), np.float32)
    for p in range(P):
        sel_z[p, DIM - CH + p // DIM] = 1
    for q in range(CH):
        for s in range(CH):
            sel_dense[DIM * s + q, q, s] = 1
    sel_emb = np.zeros((P, 2 * P - DIM), np.float32)
    for p in range(H):
        sel_emb[p, P - DIM + p % DIM] = 1
    row_of = np.arange(P * KT, dtype=np.float32).reshape(P, KT)
    return np.eye(P, dtype=np.float32), sel_z, sel_dense, sel_emb, np.concatenate([row_of, -row_of], axis=1)


def kernel(**inputs):
    import concourse.bacc as _bacc
    from concourse.bass_utils import run_bass_kernel_spmd as _run

    given = {name: np.asarray(a) for name, a in inputs.items()}
    m_raw, w1, dense_t = layouts(given["W_top1"], given["dense_ctx"], given["L0_rec_bilinear_matrices"])
    ident, sel_z, sel_dense, sel_emb, row_of = selectors()
    laid = {"ids": given["ids"], "ids_rows": given["ids"].T[LOOKED].reshape(len(LOOKED) // 2, 2 * BATCH)}
    laid["small"] = small_tables([given[f"tbl_{f}"] for f in LOOKED])
    for f in GATHERED_FIELDS:
        laid[f"tbl_{f}"] = given[f"tbl_{f}"]
    laid["m_raw"] = m_raw
    laid["w1"] = w1
    laid["b1"] = given["b_top1"].reshape(NB1, P).T
    laid["w2"] = given["W_top2"]
    laid["b2"] = given["b_top2"].reshape(NB2, P).T
    laid["w3"] = given["W_top3"].reshape(NB2, P).T
    laid["dense_t"] = dense_t
    laid["ident"] = ident
    laid["sel_z"] = sel_z
    laid["sel_dense"] = sel_dense
    laid["sel_emb"] = sel_emb
    laid["row_of"] = row_of

    nc = _bacc.Bacc("TRN2", target_bir_lowering=False, num_devices=1)
    arrays, aps = {}, {}
    for name, a in laid.items():
        a = np.ascontiguousarray(a)
        arrays[f"in_{name}"] = a
        aps[name] = nc.dram_tensor(f"in_{name}", a.shape, mybir.dt.from_np(a.dtype), kind="ExternalInput").ap()
    out = nc.dram_tensor("out_0", (BATCH, 1), F32, kind="ExternalOutput").ap()
    build(nc, aps["ids"], aps["ids_rows"], aps["small"], aps["row_of"],
          {f: aps[f"tbl_{f}"] for f in GATHERED_FIELDS}, aps["m_raw"], aps["w1"], aps["b1"], aps["w2"],
          aps["b2"], aps["w3"], aps["dense_t"], aps["ident"], aps["sel_z"], aps["sel_dense"], aps["sel_emb"], out)
    r = _run(nc, [arrays], core_ids=[0])
    return r.results[0]["out_0"]
```
